# Optimizing a Trainium2 kernel written in Bass

```python
import numpy as np
import jax
import jax.numpy as jnp

def _softmax(x, axis=-1):
    return jax.nn.softmax(x, axis=axis)

def _gelu(x):
    return jax.nn.gelu(x, approximate=True)

def _silu(x):
    return jax.nn.silu(x)

def _sigmoid(x):
    return jax.nn.sigmoid(x)

def _layernorm(x, axis=-1, eps=1e-05):
    m = jnp.mean(x, axis=axis, keepdims=True)
    v = jnp.var(x, axis=axis, keepdims=True)
    return (x - m) / jnp.sqrt(v + eps)

def _scatter_add(tgt, idx, src, axis=0):
    return tgt.at[idx].add(src)

def _segment_sum(src, seg, n):
    return jax.ops.segment_sum(src, seg, n)
kernel_name = 'mk_recurrent_d1_jaxref_r8_f9e0ab'

def setup_inputs(seed: int=0):
    np.random.seed(seed)
    _w = jnp.asarray

    def _L0_attn_setup():
        import jax, jax.numpy as jnp
        import numpy as np
        B, S, D, H = (2, 256, 128, 16)
        HD = D // H
        key = jax.random.key(seed)
        ks = jax.random.split(key, 5)
        x = jax.random.normal(ks[0], (B, S, D), dtype=jnp.float32)
        qk_w = jax.random.normal(ks[1], (D, 2 * D), dtype=jnp.float32) * 0.02
        qk_b = jnp.zeros((2 * D,), dtype=jnp.float32)
        v_w = jax.random.normal(ks[2], (D, D), dtype=jnp.float32) * 0.02
        cproj_w = jax.random.normal(ks[3], (D, D), dtype=jnp.float32) * 0.02
        resid_gain = jnp.ones((1, H, 1, 1), dtype=jnp.float32)
        skip_gain = jnp.ones((1, H, 1, 1), dtype=jnp.float32)
        centre_gain = jnp.ones((1, H, 1, 1), dtype=jnp.float32)
        return {'x': x, 'qk_w': qk_w, 'qk_b': qk_b, 'v_w': v_w, 'cproj_w': cproj_w, 'resid_gain': resid_gain, 'skip_gain': skip_gain, 'centre_gain': centre_gain}
    _L0_attn_in = _L0_attn_setup()

    def _L0_ffn_setup():
        import jax, jax.numpy as jnp
        import numpy as np
        CAPACITY_FACTOR = 1.25
        key = jax.random.key(seed)
        k1, k2, k3, k4 = jax.random.split(key, 4)
        B, S, D, E, H = (2, 256, 128, 16, 512)
        inputs = jax.random.normal(k1, (B, S, D), dtype=jnp.float32)
        gate_w = jax.random.normal(k2, (E, D), dtype=jnp.float32) / np.float32(np.sqrt(D))
        w1 = jax.random.normal(k3, (E, D, H), dtype=jnp.float32) / np.float32(np.sqrt(D))
        w2 = jax.random.normal(k4, (E, H, D), dtype=jnp.float32) / np.float32(np.sqrt(H))
        return {'inputs': inputs, 'gate_w': gate_w, 'w1': w1, 'w2': w2}
    _L0_ffn_in = _L0_ffn_setup()
    _d = {'L0_attn_x': _L0_attn_in['x'], 'L0_attn_qk_w': _L0_attn_in['qk_w'], 'L0_attn_qk_b': _L0_attn_in['qk_b'], 'L0_attn_v_w': _L0_attn_in['v_w'], 'L0_attn_cproj_w': _L0_attn_in['cproj_w'], 'L0_attn_resid_gain': _L0_attn_in['resid_gain'], 'L0_attn_skip_gain': _L0_attn_in['skip_gain'], 'L0_attn_centre_gain': _L0_attn_in['centre_gain'], 'L0_ffn_gate_w': _L0_ffn_in['gate_w'], 'L0_ffn_w1': _L0_ffn_in['w1'], 'L0_ffn_w2': _L0_ffn_in['w2']}
    _x0 = _d['L0_attn_x']
    _d['L0_attn_x'] = jax.random.normal(jax.random.fold_in(jax.random.key(seed), 1), (4, 512, 128), dtype=_x0.dtype)
    del _x0
    return _d

def reference(L0_attn_x, L0_attn_qk_w, L0_attn_qk_b, L0_attn_v_w, L0_attn_cproj_w, L0_attn_resid_gain, L0_attn_skip_gain, L0_attn_centre_gain, L0_ffn_gate_w, L0_ffn_w1, L0_ffn_w2):

    def _L0_attn_ref(x, qk_w, qk_b, v_w, cproj_w, resid_gain, skip_gain, centre_gain):
        import jax, jax.numpy as jnp
        import numpy as np
        B, S, D, H = (2, 256, 128, 16)
        HD = D // H
        b, s, d = x.shape
        h, hd = (H, d // H)
        qk = x @ qk_w + qk_b
        q, k = jnp.split(qk, 2, axis=-1)
        v = x @ v_w
        q = q.reshape(b, s, h, hd).transpose(0, 2, 1, 3)
        k = k.reshape(b, s, h, hd).transpose(0, 2, 1, 3)
        v = v.reshape(b, s, h, hd).transpose(0, 2, 1, 3)
        scores = jnp.einsum('bhqd,bhkd->bhqk', q, k) / jnp.sqrt(jnp.float32(hd))
        causal = jnp.tril(jnp.ones((s, s), dtype=bool))
        neg = jnp.finfo(scores.dtype).min
        scores = jnp.where(causal, scores, neg)
        attn = jax.nn.softmax(scores, axis=-1)
        row = jnp.arange(1, s + 1, dtype=jnp.float32)
        uniform = jnp.tril(jnp.ones((s, s), dtype=jnp.float32) / row[:, None])
        eye = jnp.eye(s, dtype=jnp.float32)
        new_attn = resid_gain * attn + skip_gain * eye[None, None] - centre_gain * uniform[None, None]
        out = jnp.einsum('bhqk,bhkd->bhqd', new_attn, v)
        out = out.transpose(0, 2, 1, 3).reshape(b, s, d)
        out = out @ cproj_w
        return out

    def _L0_ffn_ref(inputs, gate_w, w1, w2):
        import jax, jax.numpy as jnp
        import numpy as np
        CAPACITY_FACTOR = 1.25
        orig_shape = inputs.shape
        D = orig_shape[-1]
        tokens = inputs.reshape(-1, D)
        T = tokens.shape[0]
        E = gate_w.shape[0]
        C = int(CAPACITY_FACTOR * T / E)
        logits = tokens @ gate_w.T
        probs = jax.nn.softmax(logits, axis=-1)
        expert_idx = jnp.argmax(probs, axis=-1)
        mask = jax.nn.one_hot(expert_idx, E, dtype=jnp.int32)
        locations = jnp.cumsum(mask, axis=0) - 1
        mask = mask * (locations < C)
        loc_oh = jax.nn.one_hot(locations, C, dtype=probs.dtype)
        sec_mask = mask[:, :, None].astype(probs.dtype) * loc_oh
        combine_weights = probs[:, :, None] * sec_mask
        dispatch = jnp.einsum('tec,td->ecd', sec_mask, tokens)
        h = jax.nn.relu(jnp.einsum('ecd,edh->ech', dispatch, w1))
        expert_out = jnp.einsum('ech,ehd->ecd', h, w2)
        ans = jnp.einsum('tec,ecd->td', combine_weights, expert_out)
        return ans.reshape(orig_shape)
    x = L0_attn_x
    xn = _layernorm(x, axis=-1)
    s = _L0_attn_ref(xn, L0_attn_qk_w, L0_attn_qk_b, L0_attn_v_w, L0_attn_cproj_w, L0_attn_resid_gain, L0_attn_skip_gain, L0_attn_centre_gain)
    g = _silu(_L0_ffn_ref(xn, L0_ffn_gate_w, L0_ffn_w1, L0_ffn_w2))
    x = x + s * g
    return x

_drawn_inputs = setup_inputs


def setup_inputs(seed=0):
    import zlib

    import numpy as np

    out = dict(_drawn_inputs(seed))
    spreads = {'L0_attn_qk_b': (0.0, 0.8),
     'L0_attn_resid_gain': (1.0, 0.6),
     'L0_attn_skip_gain': (1.0, 0.6),
     'L0_attn_centre_gain': (1.0, 0.6)}
    factors = {'L0_attn_qk_w': 8.0,
     'L0_attn_v_w': 8.0,
     'L0_attn_cproj_w': 8.0,
     'L0_ffn_gate_w': 8.0,
     'L0_ffn_w1': 8.0,
     'L0_ffn_w2': 8.0}
    for name, (base, spread) in spreads.items():
        noise = np.random.default_rng([zlib.crc32(name.encode()), seed]).standard_normal(out[name].shape)
        drawn = base * np.exp(spread * noise) if base else spread * noise
        out[name] = jnp.asarray(drawn.astype(out[name].dtype))
    for name, factor in factors.items():
        out[name] = (out[name] * factor).astype(out[name].dtype)
    return out
```

```python
from contextlib import ExitStack

import numpy as np

import concourse.bass as bass
from concourse import mybir

F32 = mybir.dt.float32
BF16 = mybir.dt.bfloat16
I32 = mybir.dt.int32
U32 = mybir.dt.uint32
ALU = mybir.AluOpType
ACT = mybir.ActivationFunctionType
AX = mybir.AxisListType

P = 128
NEG = -1.0e30
ONE_ONE = float(np.array([0x3F803F80], np.uint32).view(np.float32)[0])
DROPPED = 1.0e6


def attention_moe_block(nc, x, qk_w, qk_b, v_w, cproj_w, resid_gain, skip_gain, centre_gain, gate_w, w1, w2, out):
    B, S, D = x.shape
    H = resid_gain.shape[1]
    HD = D // H
    E, _, F = w1.shape
    T = B * S
    CAP = int(1.25 * T / E)
    NT = T // P
    QT = S // P
    G = 4
    NG = H // G
    FC = F // P
    SLOTS = E * CAP
    SB = SLOTS // P
    PAIRS = 6
    R = PAIRS * HD
    MR = R + 3
    S1N = 2 * G + G // 2 + 1
    S2N = 2 * G + G // 2
    VB = (NT + 2) // 3
    WR = 3
    PART_PAIRS = ((0, 0), (0, 1), (1, 0), (1, 1), (0, 2), (2, 0))
    SCALE = float(HD) ** -0.5
    assert D == P and S == 4 * P and HD == 8 and H == 16 and SLOTS % P == 0

    K = B * NG
    LAG = 2
    STAGES = range(-LAG, K)
    SILU_AT = 13
    tasks = {}

    def place(kind, arg, stage, step):
        tasks.setdefault((stage, step), []).append((kind, arg))

    V_AHEAD = VB
    for i in range(V_AHEAD, VB):
        place("v", i, -2, i + 1)
    place("route_a", 0, -2, 2)
    place("route_b", 0, -2, 5)
    place("qk", 1, 0, 3)
    place("qk_low", 1, 0, 4)
    place("place", 1, 0, 4)
    for b in range(2, B):
        place("qk", b, (b - 1) * NG - 1, 3)
        place("qk_low", b, (b - 1) * NG - 1, 4)
        place("place", b, (b - 1) * NG, 4)
    for k in range(K):
        place("maxT", k, k - 1, 1)
        place("max_low", k, k - 1, 2)
    for k in range(1, K):
        for kb, step in enumerate((0, 2, 4, 5)):
            place("weigh", (k - 1, kb), k, step)
        place("copy_o", k - 1, k, 6)
        place("oT", k - 1, k, 8)
    for b in range(B):
        place("cum", b, b * NG, 9)
    place("slots_load", 0, 1, 4)
    for i in range(SB // 4):
        place("slotT", i, 2, 5 + i)
    at = 3
    for stage, n in zip(range(3, 9), (3, 3, 3, 3, 2, 2)):
        for j in range(n):
            e = at - 3
            at += 1
            step = j * 8 // n
            place("hid", (e, 0), stage, step)
            place("hid", (e, 1), stage, step + 1)
            place("res", e, stage, step + 3)
    for i in range(SB // 4):
        place("resT", i, 9, 1 + i)
    GATHER_AT = {10: range(0, NT // 2), 11: range(NT // 2, NT)}
    place("attT", 0, SILU_AT, ("late", 4))
    place("proj", 0, SILU_AT, ("late", 8))
    for b in range(1, B - 1):
        place("attT", b, K - 3 + b, 3)
        place("proj", b, K - 3 + b, 7)

    def stage_order(k):
        order, late = [], []
        for i in range(S1N):
            if k >= 0 and i < S2N:
                order.append(("s2", i))
            if k + LAG < K:
                (late if k == SILU_AT else order).append(("s1", i))
            order += tasks.get((k, i), ())
            late += tasks.get((k, ("late", i)), ())
        if k == SILU_AT:
            order.append(("silu", 0))
        return order + late

    orders = {k: stage_order(k) for k in STAGES}

    uses = ["columns", "xT0", "q0", "k0"] + [f"xT{b}" for b in range(1, B)] + [f"v{i}" for i in range(V_AHEAD)]
    for k in STAGES:
        for kind, arg in orders[k]:
            if kind == "qk":
                uses += [f"q{arg}", f"k{arg}"]
            elif kind == "hid":
                uses.append(f"hid{arg[0]}_{arg[1]}")
            elif kind == "route_b":
                uses.append("route")
            elif kind in ("v", "maxT", "slotT", "res", "resT", "oT", "cum", "attT", "proj"):
                uses.append(f"{kind}{arg}")
    uses += [f"oT{K - 1}", f"attT{B - 1}", f"proj{B - 1}"]
    use_of = {name: n for n, name in enumerate(uses)}

    with ExitStack() as ctx:
        def sb(name, shape, dt=F32):
            return ctx.enter_context(nc.sbuf_tensor(name, shape, dt))

        def sem(name):
            return ctx.enter_context(nc.semaphore(name))

        def dram(name, shape, dt):
            return nc.dram_tensor(name, shape, dt, kind="Internal").ap()

        max_rows = dram("max_rows", [K, 3, G, S], BF16)
        slot_rows = dram("slot_rows", [SLOTS, D], F32)
        result_rows = dram("result_rows", [SLOTS, D], F32)

        stack = sb("stack", [P, 2, H, 2, S], BF16)
        qs, ks = stack[:, :, :, 0, :], stack[:, :, :, 1, :]
        probs = sb("probs", [P, 2, S2N, S])
        x_sb = sb("x_sb", [P, NT, D])
        xn = sb("xn", [P, NT, D])
        fg = xn
        slot_xT = sb("slot_xT", [P, SLOTS])
        slot_sb = sb("slot_sb", [P, SB, D])
        v_aug = sb("v_aug", [P, NT, H, HD + 1])
        v_pre = sb("v_pre", [P, 2, D])
        w1_sb = sb("w1_sb", [P, WR, F])
        w2_sb = sb("w2_sb", [P, WR, FC, D])
        hid = sb("hid", [P, 2, FC, CAP])
        parts = sb("parts", [P, 2, 3, S], BF16)
        rest = sb("rest", [P, 2, S])
        attn = sb("attn", [P, NT, D])
        xnT = [slot_xT[:, b * S:(b + 1) * S] for b in range(2)]
        xnT += [attn[:, b * QT:(b + 1) * QT, :].rearrange("p t d -> p (t d)") for b in range(2, B)]
        warm = sb("warm", [P, 1])
        oT_sb = sb("oT_sb", [P, 2, S])
        att_T = sb("att_T", [P, S])
        y_sb = rest
        wqk = sb("wqk", [P, 2, HD, H])
        wqk_raw = att_T[:, 0:2 * D]
        brow_raw = att_T[0:1, 2 * D:4 * D]
        wvg = sb("wvg", [P, D + E])
        wc = sb("wc", [P, D])
        gate_sb = sb("gate_sb", [E, D])
        brow = sb("brow", [1, 2, HD, H])
        bias = sb("bias", [P, 2])
        gains = sb("gains", [P, 3, H])
        identf = sb("identf", [P, P])
        identb = sb("identb", [P, P], BF16)
        maskneg = sb("maskneg", [P, P], BF16)
        before = sb("before", [P, P], BF16)
        onesb = sb("onesb", [P, P], BF16)
        upto = sb("upto", [P, P])
        onesf = sb("onesf", [P, P])
        stats = sb("stats", [P, NT, 6])
        mv = sb("mv", [P, NT, 2])
        rstd = sb("rstd", [P, 4, NT])
        lg = sb("lg", [P, NT, E])
        rt = oT_sb[:, :, :].rearrange("p a t -> p (a t)")[:, 0:3 * NT * E].rearrange("p (a t e) -> p a t e", a=3, t=NT)
        rtc = sb("rtc", [P, 8, NT])
        onehot = sb("onehot", [P, NT, E], BF16)
        ev = sb("ev", [P, E])
        idx = sb("idx", [P, NT], I32)
        row_i = sb("row_i", [P, QT], I32)
        inv_row = sb("inv_row", [P, 2, QT])
        mx = sb("mx", [P, 2, G, QT])
        negm = sb("negm", [G * QT, 2, 3, P], BF16)
        mrest = sb("mrest", [G * QT, P])
        rec = sb("rec", [P, QT, G])
        recg = sb("recg", [P, QT, G])
        onorm = sb("onorm", [P, QT, G, HD])
        cum_gain = sb("cum_gain", [P, QT, H])
        cum_part = sb("cum_part", [P, QT, H, HD])

        def bank(name):
            return ctx.enter_context(nc.psum_tensor(name, [P, 512], F32))

        s1_bank = [bank(f"s1_bank{i}") for i in range(2)]
        s2_bank = [bank(f"s2_bank{i}") for i in range(3)]
        o_bank = bank("o_bank")
        mi_bank = [bank(f"mi_bank{i}") for i in range(2)]

        x_loaded = [sem(f"x_loaded{b}") for b in range(B)]
        small_loaded = sem("small_loaded")
        wqk_loaded = sem("wqk_loaded")
        wv_loaded = sem("wv_loaded")
        brow_turned = sem("brow_turned")
        wqk_turned = sem("wqk_turned")
        wc_loaded = sem("wc_loaded")
        gains_loaded = sem("gains_loaded")
        const_step = sem("const_step")
        consts_ready = sem("consts_ready")
        q_filled = [sem(f"q_filled{i}") for i in range(2)]
        k_filled = sem("k_filled")
        slots_filled = sem("slots_filled")
        o_filled = sem("o_filled")
        ones_filled = sem("ones_filled")
        ln_step = sem("ln_step")
        var_ready = sem("var_ready")
        std_ready = sem("std_ready")
        rstd_ready = sem("rstd_ready")
        xn_ready = [sem(f"xn_ready{b}") for b in range(B)]
        mi_full = [sem(f"mi_full{i}") for i in range(2)]
        mi_free = [sem(f"mi_free{i}") for i in range(2)]
        wvg_ready = sem("wvg_ready")
        hi_ready = sem("hi_ready")
        mid_ready = sem("mid_ready")
        lo_ready = sem("lo_ready")
        parts_placed = [sem(f"parts_placed{b}") for b in range(B)]
        v_ready = sem("v_ready")
        vpre_ready = sem("vpre_ready")
        route_step = sem("route_step")
        onehot_ready = sem("onehot_ready")
        gate_shift_ready = sem("gate_shift_ready")
        gate_exp_ready = sem("gate_exp_ready")
        prob_ready = sem("prob_ready")
        idx_ready = sem("idx_ready")
        slots_cleared = sem("slots_cleared")
        scattered = sem("scattered")
        slots_loaded = sem("slots_loaded")
        w_ring = [sem(f"w_ring{i}") for i in range(WR)]
        results_stored = sem("results_stored")
        fg_cleared = sem("fg_cleared")
        gathered = sem("gathered")
        silu_ready = sem("silu_ready")
        s1_full = sem("s1_full")
        s1_free = sem("s1_free")
        s2_full = sem("s2_full")
        s2_free = sem("s2_free")
        masked = sem("masked")
        weighed = sem("weighed")
        o_copied = sem("o_copied")
        nm_hi_ready = sem("nm_hi_ready")
        nm_mid_ready = sem("nm_mid_ready")
        nm_lo_ready = sem("nm_lo_ready")
        max_stored = [sem(f"max_stored{i}") for i in range(2)]
        max_placed = [sem(f"max_placed{i}") for i in range(2)]
        cum_gain_step = sem("cum_gain_step")
        skip_ready = sem("skip_ready")
        base_ready = sem("base_ready")
        norm_step = sem("norm_step")
        attn_ready = sem("attn_ready")
        gated_ready = sem("gated_ready")
        y_ready = sem("y_ready")
        y_stored = [sem(f"y_stored{i}") for i in range(2)]

        def take(name):
            n = use_of[name]
            if n >= 2:
                nc.tensor.wait_ge(mi_free[n % 2], n // 2)
            return mi_bank[n % 2]

        def full(name):
            return mi_full[use_of[name] % 2]

        def free(name):
            return mi_free[use_of[name] % 2]

        def wait_full(eng, name):
            eng.wait_ge(full(name), use_of[name] // 2 + 1)
            return mi_bank[use_of[name] % 2]

        def wait_free(eng, name):
            eng.wait_ge(free(name), use_of[name] // 2 + 1)

        def wait_x_turned(eng, b):
            wait_free(eng, f"xT{b}")

        def placed_dmas(b):
            return PAIRS + (1 if b >= 2 else 0)

        def query_blocks(g, i):
            if i < 2 * G:
                return [(g * G + i % G, QT - 1 - i // G)]
            if i < S1N - 1:
                return [(g * G + 2 * (i - 2 * G) + j, 1) for j in range(2)]
            return [(g * G + j, 0) for j in range(G)]

        def normalise_x(eng, engine, b):
            eng.wait_ge(rstd_ready, 2 if b else 1)
            for t in range(b * QT, (b + 1) * QT):
                ins = engine.tensor_scalar(xn[:, t, :], x_sb[:, t, :], mv[:, t, 0:1], rstd[:, 0, t:t + 1],
                                           ALU.subtract, ALU.mult)
            ins.then_inc(xn_ready[b], 1)

        block = ctx.enter_context(nc.Block())

        @block.sync
        def _(sp):
            for b in range(B):
                sp.dma_start(x_sb[:, b * QT:(b + 1) * QT, :], x[b].rearrange("(t p) d -> p t d", p=P))\
                    .then_inc(x_loaded[b], 16)
            sp.dma_start(wvg[:, 0:D], v_w).then_inc(wv_loaded, 16)
            sp.dma_start(wc[:, :], cproj_w).then_inc(wc_loaded, 16)
            for i, gain in enumerate((resid_gain, skip_gain, centre_gain)):
                sp.dma_start(gains[:, i, :], gain.rearrange("a h b c -> (a b c) h").to_broadcast([P, H]))\
                    .then_inc(gains_loaded, 16)

            by_part = parts[:, :, :, :].rearrange("p i c t -> p (i c) t")

            def place_parts(b):
                par = b % 2
                if b >= 2:
                    sp.wait_ge(s2_full, (b - 1) * NG * S2N)
                    sp.dma_start(qs[R:MR, par], qs[64:64 + MR - R, par]).then_inc(parts_placed[b], 16)
                else:
                    sp.wait_ge(q_filled[b], 1)
                    sp.wait_ge(k_filled, b + 1)
                for row, (cq, ck) in enumerate(PART_PAIRS):
                    if row == 0:
                        sp.wait_ge(hi_ready, 2 * b + 2)
                    elif row == 1:
                        sp.wait_ge(mid_ready, 2 * b + 2)
                    elif row == 4:
                        sp.wait_ge(lo_ready, 2 * b + 2)
                    rows = slice(row * HD, (row + 1) * HD)
                    sp.dma_start(stack[rows, par], by_part[:, cq:4 + ck:3 + ck - cq, :]).then_inc(parts_placed[b], 16)

            def load_expert(e):
                if e >= WR:
                    wait_full(sp, f"res{e - WR}")
                sp.dma_start(w1_sb[:, e % WR, :], w1[e]).then_inc(w_ring[e % WR], 16)
                sp.dma_start(w2_sb[:, e % WR], w2[e].rearrange("(c p) d -> p c d", p=P)).then_inc(w_ring[e % WR], 16)

            def place_max(k):
                sp.wait_ge(nm_lo_ready, k + 1)
                b, g = divmod(k, NG)
                sp.dma_start(max_rows[k].rearrange("c h (t q) -> (h t) c q", q=P), negm[:, k % 2]).then_inc(max_stored[k % 2], 16)
                sp.wait_ge(max_stored[k % 2], 16 * (k // 2 + 1))
                sp.dma_start(stack[R:MR, b % 2, g * G:(g + 1) * G, 0, :], max_rows[k]).then_inc(max_placed[k % 2], 16)

            def store_y(b):
                sp.wait_ge(y_ready, b + 1)
                sp.dma_start(out[b].rearrange("(t p) d -> p t d", p=P),
                             y_sb[:, b % 2, :].rearrange("p (t d) -> p t d", t=QT)).then_inc(y_stored[b % 2], 16)

            place_parts(0)
            sp.wait_ge(slots_filled, 1)
            sp.dma_start(slot_rows.rearrange("(k p) d -> p k d", p=P), slot_sb[:, :, :]).then_inc(slots_cleared, 16)
            for e in range(WR):
                load_expert(e)
            for k in STAGES:
                for kind, arg in orders[k]:
                    if kind == "max_low":
                        place_max(arg)
                    elif kind == "place":
                        place_parts(arg)
                    elif kind == "slots_load":
                        sp.wait_ge(scattered, 16 * NT)
                        sp.dma_start(slot_sb[:, :, :], slot_rows.rearrange("(k p) d -> p k d", p=P))\
                            .then_inc(slots_loaded, 16)
                    elif kind == "res" and arg + WR < E:
                        load_expert(arg + WR)
                    elif kind == "resT" and arg == SB // 4 - 1:
                        for i in range(SB // 4):
                            wait_free(sp, f"resT{i}")
                        sp.dma_start(result_rows.rearrange("(k p) d -> p k d", p=P), slot_sb[:, :, :])\
                            .then_inc(results_stored, 16)
                    elif kind == "proj":
                        store_y(arg)
            store_y(B - 1)
            for i in range(2):
                sp.wait_ge(y_stored[i], 16 * (B // 2))

        @block.gpsimd
        def _(pool):
            nc.gpsimd.memset(identf[:, :], 0.0).then_inc(const_step, 1)
            nc.gpsimd.memset(onesf[:, :], 1.0).then_inc(const_step, 1)
            nc.gpsimd.memset(onesb[:, :], 1.0).then_inc(const_step, 1)
            nc.gpsimd.memset(maskneg[:, :], 0.0).then_inc(const_step, 1)
            pool.wait_ge(const_step, 4)
            nc.gpsimd.affine_select(out=identf[:, :], in_=identf[:, :], compare_op=ALU.not_equal, fill=1.0,
                                    base=0, pattern=[[-1, P]], channel_multiplier=1).then_inc(const_step, 1)
            nc.gpsimd.affine_select(out=maskneg[:, :], in_=maskneg[:, :], compare_op=ALU.is_ge, fill=NEG,
                                    base=0, pattern=[[-1, P]], channel_multiplier=1)
            pool.wait_ge(const_step, 5)
            nc.gpsimd.tensor_copy(identb[:, :], identf[:, :]).then_inc(consts_ready, 1)
            nc.gpsimd.memset(ks[:, 0].bitcast(F32), ONE_ONE).then_inc(k_filled, 1)
            nc.gpsimd.memset(qs[:, 0].bitcast(F32), 0.0).then_inc(q_filled[0], 1)
            nc.gpsimd.affine_select(out=before[:, :], in_=onesb[:, :], compare_op=ALU.is_gt, fill=0.0,
                                    base=0, pattern=[[1, P]], channel_multiplier=-1)
            nc.gpsimd.affine_select(out=upto[:, :], in_=onesf[:, :], compare_op=ALU.is_ge, fill=0.0,
                                    base=0, pattern=[[1, P]], channel_multiplier=-1)
            nc.gpsimd.iota(ev[:, :], [[1, E]], base=-E, channel_multiplier=0,
                           allow_small_or_imprecise_dtypes=True)
            nc.gpsimd.iota(row_i[:, :], [[P, QT]], base=1, channel_multiplier=1).then_inc(consts_ready, 1)
            nc.gpsimd.memset(v_aug[:, :, :, HD:HD + 1], 1.0).then_inc(ones_filled, 1)
            for b in range(2, B):
                normalise_x(pool, nc.gpsimd, b)
            nc.gpsimd.memset(slot_sb[:, :, :], 0.0).then_inc(slots_filled, 1)
            nc.gpsimd.memset(qs[:, 1].bitcast(F32), 0.0).then_inc(q_filled[1], 1)
            nc.gpsimd.memset(ks[:, 1].bitcast(F32), ONE_ONE).then_inc(k_filled, 1)

            def scatter():
                pool.wait_ge(idx_ready, 1)
                pool.wait_ge(slots_cleared, 16)
                for t in range(NT):
                    pool.indirect_dma_start(
                        slot_rows, bass.IndirectOffsetOnAxis(ap=idx[:, t:t + 1].bitcast(U32), axis=0),
                        xn[:, t, :], None, bounds_check=SLOTS - 1, oob_is_err=False).then_inc(scattered, 16)

            def gather(t):
                pool.indirect_dma_start(
                    fg[:, t, :], None, result_rows,
                    bass.IndirectOffsetOnAxis(ap=idx[:, t:t + 1].bitcast(U32), axis=0),
                    bounds_check=SLOTS - 1, oob_is_err=False).then_inc(gathered, 16)

            def prefix_values(b):
                if b == 0:
                    pool.wait_ge(v_ready, VB)
                    pool.wait_ge(gains_loaded, 48)
                else:
                    wait_full(pool, f"cum{b - 1}")
                    if b >= 2:
                        wait_full(pool, f"k{b}")
                va = v_aug[:, b * QT:(b + 1) * QT, :, 0:HD]
                pre = v_pre[:, :, :].rearrange("p t (h d) -> p t h d", h=H)
                nc.gpsimd.tensor_tensor(pre[:, 0], va[:, 0], va[:, 1], ALU.add).then_inc(vpre_ready, 1)
                pool.wait_ge(vpre_ready, 2 * b + 1)
                nc.gpsimd.tensor_tensor(pre[:, 1], pre[:, 0], va[:, 2], ALU.add).then_inc(vpre_ready, 1)
                for t in range(QT):
                    ins = nc.gpsimd.tensor_tensor(
                        attn[:, b * QT + t, :].rearrange("p (h d) -> p h d", h=H), va[:, t],
                        gains[:, 1, :].rearrange("p (h o) -> p h o", o=1).to_broadcast([P, H, HD]), ALU.mult)
                ins.then_inc(skip_ready, 1)

            def mask_probs(k, tokens):
                par = k % 2
                blocks = probs[:, par, :, :].rearrange("p u (c q) -> p (u c) q", q=P)
                for n, first, apart in ((G, 0, QT), (2 * G, G * QT, QT), (2 * G, G * QT + 3, QT), (S2N, 2 * G * QT, 2)):
                    pool.wait_ge(s2_free, k * S2N + n)
                    v = blocks[:, first:first + apart * (G - 1) + 1:apart, :]
                    nc.gpsimd.affine_select(out=v, in_=v, compare_op=ALU.is_ge, fill=0.0, base=0,
                                            pattern=[[0, G], [1, P]], channel_multiplier=-1).then_inc(masked, 1)
                    for t in tokens[:2]:
                        gather(t)
                    tokens = tokens[2:]

            prefix_values(0)
            scatter()
            pool.wait_ge(scattered, 16 * NT)
            nc.gpsimd.memset(fg[:, :, :], 0.0).then_inc(fg_cleared, 1)
            for k in range(K):
                if k % NG == 1 and k // NG + 1 < B:
                    prefix_values(k // NG + 1)
                if k == min(GATHER_AT):
                    pool.wait_ge(fg_cleared, 1)
                    pool.wait_ge(results_stored, 16)
                mask_probs(k, GATHER_AT.get(k, range(0)))

        @block.scalar
        def _(act):
            act.dma_start(wqk_raw, qk_w).then_inc(wqk_loaded, 16)
            act.dma_start(gate_sb[:, :], gate_w).then_inc(small_loaded, 16)
            act.dma_start(brow_raw, qk_b.rearrange("(o n) -> o n", o=1)).then_inc(small_loaded, 16)
            act.wait_ge(const_step, 4)
            nc.scalar.activation(warm[:, :], onesf[:, 0:1], ACT.Sqrt)
            act.wait_ge(small_loaded, 32)
            nc.scalar.activation(brow[:, :, :, :], brow_raw.rearrange("o (i h d) -> o i d h", i=2, h=H), ACT.Copy)\
                .then_inc(brow_turned, 1)
            act.wait_ge(wqk_loaded, 16)
            nc.scalar.activation(wqk[:, :, :, :], wqk_raw.rearrange("p (i h d) -> p i d h", i=2, h=H), ACT.Copy)\
                .then_inc(wqk_turned, 1)

            def deviation(turn):
                act.wait_ge(var_ready, turn + 1)
                ts = slice(turn * QT, NT if turn else QT)
                nc.scalar.activation(rstd[:, 1, ts], rstd[:, 0, ts], ACT.Sqrt).then_inc(std_ready, 1)

            def copy_xT(b):
                m = wait_full(act, f"xT{b}")
                nc.scalar.activation(xnT[b], m[:, :], ACT.Copy).then_inc(free(f"xT{b}"), 1)

            def split_hi(b):
                if b:
                    act.wait_ge(parts_placed[b - 1], 16 * placed_dmas(b - 1))
                else:
                    wait_free(act, "columns")
                for i, n in enumerate("qk"):
                    m = wait_full(act, f"{n}{b}")
                    nc.scalar.activation(parts[:, i, 0, :], m[:, :], ACT.Identity,
                                         bias=bias[:, i:i + 1]).then_inc(hi_ready, 1)

            def split_mid(b):
                for i, n in enumerate("qk"):
                    wait_free(act, f"{n}{b}")
                    nc.scalar.activation(parts[:, i, 1, :], rest[:, i, :], ACT.Copy).then_inc(mid_ready, 1)

            deviation(0)
            m = wait_full(act, "columns")
            nc.scalar.activation(wvg[:, D:D + E], m[:, 0:E], ACT.Copy).then_inc(wvg_ready, 1)
            nc.scalar.activation(bias[:, :], m[:, E:E + 2], ACT.Copy).then_inc(free("columns"), 1)
            deviation(1)
            copy_xT(0)
            split_hi(0)
            split_mid(0)
            for b in range(1, B):
                copy_xT(b)
            act.wait_ge(ones_filled, 1)

            def copy_values(i):
                m = wait_full(act, f"v{i}")
                n = min(3, NT - 3 * i)
                vg = m[:, 0:n * (D + E)].rearrange("p (t c) -> p t c", t=n)
                nc.scalar.activation(v_aug[:, 3 * i:3 * i + n, :, 0:HD],
                                     vg[:, :, 0:D].rearrange("p t (h d) -> p t h d", h=H), ACT.Copy).then_inc(v_ready, 1)
                nc.scalar.activation(lg[:, 3 * i:3 * i + n, :], vg[:, :, D:D + E], ACT.Copy).then_inc(free(f"v{i}"), 1)

            for i in range(V_AHEAD):
                copy_values(i)

            def exponential(k, i):
                n = k * S2N + i
                if i == 0 and k >= 2:
                    act.wait_ge(weighed, k - 1)
                act.wait_ge(s2_full, n + 1)
                nc.scalar.activation(probs[:, k % 2, i, :], s2_bank[n % 3][:, :], ACT.Exp,
                                     scale=SCALE).then_inc(s2_free, 1)

            def copy_o(k):
                act.wait_ge(weighed, k + 1)
                if k >= 2:
                    wait_full(act, f"oT{k - 2}")
                nc.scalar.activation(oT_sb[:, k % 2, :], o_bank[:, :], ACT.Copy).then_inc(o_copied, 1)

            def copy_attT(b):
                m = wait_full(act, f"attT{b}")
                nc.scalar.activation(att_T[:, :], m[:, :], ACT.Copy).then_inc(free(f"attT{b}"), 1)

            def part(k, kind, arg):
                if kind == "s2":
                    exponential(k, arg)
                elif kind == "v":
                    copy_values(arg)
                elif kind == "route_a":
                    act.wait_ge(gate_shift_ready, 1)
                    nc.scalar.activation(rt[:, 1], rt[:, 0], ACT.Exp).then_inc(gate_exp_ready, 1)
                elif kind == "qk":
                    split_hi(arg)
                elif kind == "qk_low":
                    split_mid(arg)
                elif kind == "slotT":
                    m = wait_full(act, f"slotT{arg}")
                    nc.scalar.activation(slot_xT[:, arg * 4 * P:(arg + 1) * 4 * P], m[:, :], ACT.Copy)\
                        .then_inc(free(f"slotT{arg}"), 1)
                elif kind == "hid":
                    e, c = arg
                    m = wait_full(act, f"hid{e}_{c}")
                    nc.scalar.activation(hid[:, e % 2, 2 * c:2 * c + 2, :],
                                         m[:, 0:2 * CAP].rearrange("p (c s) -> p c s", c=2), ACT.Relu)\
                        .then_inc(free(f"hid{e}_{c}"), 1)
                elif kind == "copy_o":
                    copy_o(arg)
                elif kind == "maxT":
                    m = wait_full(act, f"maxT{arg}")
                    if arg >= 2:
                        act.wait_ge(max_stored[arg % 2], 16 * (arg // 2))
                    nc.scalar.activation(negm[:, arg % 2, 0, :], m[0:G * QT, 0:P], ACT.Copy, scale=-1.0)\
                        .then_inc(nm_hi_ready, 1)
                elif kind == "max_low":
                    wait_free(act, f"maxT{arg}")
                    nc.scalar.activation(negm[:, arg % 2, 1, :], mrest[:, :], ACT.Copy).then_inc(nm_mid_ready, 1)
                elif kind == "silu":
                    act.wait_ge(gathered, 16 * NT)
                    act.wait_ge(prob_ready, 1)
                    for t in range(NT):
                        nc.scalar.activation(fg[:, t, :], fg[:, t, :], ACT.Silu, scale=rtc[:, 2, t:t + 1])\
                            .then_inc(silu_ready, 1)
                elif kind == "attT":
                    copy_attT(arg)

            for k in STAGES:
                for kind, arg in orders[k]:
                    part(k, kind, arg)
            copy_o(K - 1)
            copy_attT(B - 1)

        @block.tensor
        def _(pe):
            pe.wait_ge(consts_ready, 1)
            pe.wait_ge(small_loaded, 32)
            m = take("columns")
            nc.tensor.transpose(m[:, 0:E], gate_sb[:, :], identf[0:E, 0:E])
            pe.wait_ge(brow_turned, 1)
            for i in range(2):
                col = brow[:, i].rearrange("o d h -> o (d h)")
                mm = nc.tensor.matmul(m[:, E + i:E + i + 1], col, identf[0:1, 0:1], start=True, stop=True,
                                      skip_group_check=True)
            mm.then_inc(full("columns"), 1)

            def turn_x(b):
                pe.wait_ge(xn_ready[b], 1)
                m = take(f"xT{b}")
                for t in range(QT):
                    mm = nc.tensor.transpose(m[:, t * P:(t + 1) * P], xn[:, b * QT + t, :], identf[:, :])
                mm.then_inc(full(f"xT{b}"), 1)

            def project_qk(b):
                for i, n in enumerate("qk"):
                    m = take(f"{n}{b}")
                    wait_x_turned(pe, b)
                    w = wqk[:, i].rearrange("p d h -> p (d h)")
                    nc.tensor.matmul(m[:, :], w, xnT[b], start=True, stop=True)\
                        .then_inc(full(f"{n}{b}"), 1)

            turn_x(0)
            pe.wait_ge(wqk_turned, 1)
            project_qk(0)
            for b in range(1, B):
                turn_x(b)

            def project_v(i):
                m = take(f"v{i}")
                if i == 0:
                    pe.wait_ge(wv_loaded, 16)
                    pe.wait_ge(wvg_ready, 1)
                for j in range(min(3, NT - 3 * i)):
                    t = 3 * i + j
                    if t % QT == 0:
                        wait_x_turned(pe, t // QT)
                    mm = nc.tensor.matmul(m[:, j * (D + E):(j + 1) * (D + E)],
                                          xnT[t // QT][:, t % QT * P:(t % QT + 1) * P], wvg[:, :],
                                          start=True, stop=True, skip_group_check=True)
                mm.then_inc(full(f"v{i}"), 1)

            for i in range(V_AHEAD):
                project_v(i)

            def count_ahead():
                pe.wait_ge(consts_ready, 2)
                pe.wait_ge(onehot_ready, 1)
                m = take("route")
                nc.tensor.matmul(m[:, 0:NT * E], before[:, :], onehot[:, :, :].rearrange("p t e -> p (t e)"),
                                 start=True, stop=False, skip_group_check=True)
                for t in range(NT - 1):
                    n = NT - 1 - t
                    mm = nc.tensor.matmul(m[:, (t + 1) * E:NT * E].rearrange("p (t e) -> p t e", e=E), onesb[:, :],
                                          onehot[:, t:t + 1, :].to_broadcast([P, n, E]), start=False,
                                          stop=(t == NT - 2), skip_group_check=True)
                mm.then_inc(full("route"), 1)

            def scores_by_query(k, i):
                b, g = divmod(k, NG)
                n = k * S1N + i
                if i == 0 and g == 0:
                    pe.wait_ge(parts_placed[b], 16 * placed_dmas(b))
                if n >= 2:
                    pe.wait_ge(s1_free, n - 1)
                pt = s1_bank[n % 2]
                blocks = query_blocks(g, i)
                w = (blocks[0][1] + 1) * P
                for j, (h, qt) in enumerate(blocks):
                    nc.tensor.matmul(pt[:, j * w:(j + 1) * w], qs[:, b % 2, h, qt * P:(qt + 1) * P],
                                     ks[:, b % 2, h, 0:w], start=(j == 0), stop=False, skip_group_check=True)
                c = len(blocks)
                diag = pt[:, 0:c * w].rearrange("p (c w) -> p c w", c=c)[:, :, w - P:w]
                neg = maskneg[:, :].rearrange("p (o k) -> p o k", o=1).to_broadcast([P, c, P])
                nc.tensor.matmul(diag, identb[:, :], neg, start=False, stop=True, skip_group_check=True)\
                    .then_inc(s1_full, 1)

            def scores_by_key(k, i):
                b, g = divmod(k, NG)
                n = k * S2N + i
                if i == 0:
                    pe.wait_ge(max_placed[k % 2], 16 * (k // 2 + 1))
                if n >= 3:
                    pe.wait_ge(s2_free, n - 2)
                pt = s2_bank[n % 3]
                h0 = g * G
                if i < G:
                    blocks = [(h0 + i, 0, 0)]
                elif i < 2 * G:
                    blocks = [(h0 + i - G, 1, 0), (h0 + i - G, 3, 3 * P)]
                else:
                    blocks = [(h0 + 2 * (i - 2 * G), 2, 0), (h0 + 2 * (i - 2 * G) + 1, 2, 2 * P)]
                for h, kb, at in blocks:
                    w = S - kb * P
                    mm = nc.tensor.matmul(pt[:, at:at + w], ks[:, b % 2, h, kb * P:(kb + 1) * P],
                                          qs[:, b % 2, h, kb * P:S], start=True, stop=True, skip_group_check=True)
                mm.then_inc(s2_full, 1)

            def probs_of(par, j, kb):
                if kb == 0:
                    return probs[:, par, j, :]
                if kb == 1:
                    return probs[:, par, G + j, 0:3 * P]
                if kb == 3:
                    return probs[:, par, G + j, 3 * P:4 * P]
                return probs[:, par, 2 * G + j // 2, (j % 2) * 2 * P:(j % 2 + 1) * 2 * P]

            def weigh_values(k, kb):
                b, g = divmod(k, NG)
                pe.wait_ge(s2_free, k * S2N + (G, 2 * G, S2N, 2 * G)[kb])
                pe.wait_ge(masked, 4 * k + (1, 2, 4, 3)[kb])
                if kb == 0:
                    if k == 0:
                        pe.wait_ge(o_filled, 1)
                    else:
                        pe.wait_ge(o_copied, k)
                for j in range(G):
                    mm = nc.tensor.matmul(o_bank[32 * j:32 * j + HD + 1, kb * P:S], v_aug[:, b * QT + kb, g * G + j, :],
                                          probs_of(k % 2, j, kb), start=(kb == 0), stop=(kb == QT - 1),
                                          skip_group_check=True)
                if kb == QT - 1:
                    mm.then_inc(weighed, 1)

            def turn_o(k):
                m = take(f"oT{k}")
                pe.wait_ge(o_copied, k + 1)
                for t in range(QT):
                    mm = nc.tensor.transpose(m[:, t * P:(t + 1) * P], oT_sb[:, k % 2, t * P:(t + 1) * P], identf[:, :])
                mm.then_inc(full(f"oT{k}"), 1)

            def sum_values(b):
                m = take(f"cum{b}")
                pe.wait_ge(vpre_ready, 2 * b + 2)
                va = v_aug[:, b * QT:(b + 1) * QT, :, 0:HD].rearrange("p t h d -> p (t h) d")
                nc.tensor.matmul(m[:, :], upto[:, :], va, start=True, stop=False, skip_group_check=True)
                nc.tensor.matmul(m[:, P:2 * P], onesf[:, :], va[:, 0:H, :], start=False, stop=False,
                                 skip_group_check=True)
                nc.tensor.matmul(m[:, 2 * P:4 * P], onesf[:, :], v_pre[:, :, :].rearrange("p t d -> p (t d)"),
                                 start=False, stop=True, skip_group_check=True).then_inc(full(f"cum{b}"), 1)

            def turn_max(k):
                m = take(f"maxT{k}")
                pe.wait_ge(s1_free, (k + 1) * S1N)
                nc.tensor.transpose(m[0:G * QT, 0:P], mx[:, k % 2].rearrange("p h t -> p (h t)"), identf[:, :])\
                    .then_inc(full(f"maxT{k}"), 1)

            def turn_blocks(name, source, at):
                m = take(name)
                for j in range(4):
                    mm = nc.tensor.transpose(m[:, j * P:(j + 1) * P], source(at + j), identf[:, :])
                mm.then_inc(full(name), 1)

            def expert_hidden(e, c):
                if c == 0:
                    pe.wait_ge(w_ring[e % WR], 32 * (e // WR + 1))
                    if e == 0:
                        for i in range(SB // 4):
                            wait_free(pe, f"slotT{i}")
                m = take(f"hid{e}_{c}")
                for j in range(2):
                    at = (2 * c + j) * P
                    mm = nc.tensor.matmul(m[:, j * CAP:(j + 1) * CAP], w1_sb[:, e % WR, at:at + P],
                                          slot_xT[:, e * CAP:(e + 1) * CAP], start=True, stop=True,
                                          skip_group_check=True)
                mm.then_inc(full(f"hid{e}_{c}"), 1)

            def expert_result(e):
                m = take(f"res{e}")
                for c in range(2):
                    wait_free(pe, f"hid{e}_{c}")
                for c in range(FC):
                    mm = nc.tensor.matmul(m[:, 0:CAP], w2_sb[:, e % WR, c, :], hid[:, e % 2, c, :],
                                          start=(c == 0), stop=(c == FC - 1))
                mm.then_inc(full(f"res{e}"), 1)

            def turn_attn(b):
                m = take(f"attT{b}")
                pe.wait_ge(attn_ready, (b + 1) * NG)
                for t in range(QT):
                    mm = nc.tensor.transpose(m[:, t * P:(t + 1) * P], attn[:, b * QT + t, :], identf[:, :])
                mm.then_inc(full(f"attT{b}"), 1)

            def project_attn(b):
                m = take(f"proj{b}")
                wait_free(pe, f"attT{b}")
                if b == 0:
                    pe.wait_ge(wc_loaded, 16)
                for t in range(QT):
                    mm = nc.tensor.matmul(m[:, t * P:(t + 1) * P], att_T[:, t * P:(t + 1) * P], wc[:, :],
                                          start=True, stop=True, skip_group_check=True)
                mm.then_inc(full(f"proj{b}"), 1)

            def part(k, kind, arg):
                if kind == "s2":
                    scores_by_key(k, arg)
                elif kind == "s1":
                    scores_by_query(k + LAG, arg)
                elif kind == "v":
                    project_v(arg)
                elif kind == "route_b":
                    count_ahead()
                elif kind == "weigh":
                    weigh_values(*arg)
                elif kind == "qk":
                    project_qk(arg)
                elif kind == "slotT":
                    pe.wait_ge(slots_loaded, 16)
                    turn_blocks(f"slotT{arg}", lambda s: slot_sb[:, s, :], 4 * arg)
                elif kind == "hid":
                    expert_hidden(*arg)
                elif kind == "res":
                    expert_result(arg)
                elif kind == "resT":
                    if arg == 0:
                        for e in (E - 2, E - 1):
                            wait_free(pe, f"res{e}")
                    turn_blocks(f"resT{arg}", lambda s: slot_xT[:, s * P:(s + 1) * P], 4 * arg)
                elif kind == "oT":
                    turn_o(arg)
                elif kind == "cum":
                    sum_values(arg)
                elif kind == "maxT":
                    turn_max(arg)
                elif kind == "attT":
                    turn_attn(arg)
                elif kind == "proj":
                    project_attn(arg)

            for k in STAGES:
                for kind, arg in orders[k]:
                    part(k, kind, arg)
            for kb in range(QT):
                weigh_values(K - 1, kb)
            turn_o(K - 1)
            turn_attn(B - 1)
            project_attn(B - 1)

        @block.vector
        def _(dve):
            ln = [0]

            def ln_count(ins):
                ln[0] += 1
                ins.then_inc(ln_step, 1)
                return ln[0]

            def deviations(batches):
                tiles = range(batches[0] * QT, (batches[-1] + 1) * QT)
                ts = slice(tiles[0], tiles[-1] + 1)
                for t in tiles:
                    if t % QT == 0:
                        dve.wait_ge(x_loaded[t // QT], 16)
                    n = ln_count(nc.vector.bn_stats(stats[:, t, :], x_sb[:, t, :]))
                first = n - len(tiles) + 1
                for j, t in enumerate(tiles):
                    dve.wait_ge(ln_step, first + j)
                    n = ln_count(nc.vector.bn_aggr(mv[:, t, :], stats[:, t, :]))
                dve.wait_ge(ln_step, n)
                turn = 0 if batches[0] == 0 else 1
                nc.vector.tensor_scalar(rstd[:, 0, ts], mv[:, ts, 1], 1e-5, None, ALU.add).then_inc(var_ready, 1)
                dve.wait_ge(std_ready, turn + 1)
                n = ln_count(nc.vector.reciprocal(rstd[:, 2, ts], rstd[:, 1, ts]))
                dve.wait_ge(ln_step, n)
                n = ln_count(nc.vector.tensor_tensor(rstd[:, 1, ts], rstd[:, 2, ts], rstd[:, 2, ts], ALU.mult))
                dve.wait_ge(ln_step, n)
                n = ln_count(nc.vector.tensor_tensor(rstd[:, 3, ts], rstd[:, 1, ts], rstd[:, 0, ts], ALU.mult))
                dve.wait_ge(ln_step, n)
                n = ln_count(nc.vector.tensor_scalar(rstd[:, 1, ts], rstd[:, 3, ts], -0.5, 1.5, ALU.mult, ALU.add))
                dve.wait_ge(ln_step, n)
                nc.vector.tensor_tensor(rstd[:, 0, ts], rstd[:, 2, ts], rstd[:, 1, ts], ALU.mult).then_inc(rstd_ready, 1)

            def split_rest(b):
                for i, n in enumerate("qk"):
                    m = wait_full(dve, f"{n}{b}")
                    dve.wait_ge(hi_ready, 2 * b + i + 1)
                    nc.vector.scalar_tensor_tensor(out=rest[:, i, :], in0=m[:, :], scalar=bias[:, i:i + 1],
                                                   in1=parts[:, i, 0, :], op0=ALU.add, op1=ALU.subtract)\
                        .then_inc(free(f"{n}{b}"), 1)

            def split_lo(b):
                for i in range(2):
                    dve.wait_ge(mid_ready, 2 * b + i + 1)
                    nc.vector.tensor_tensor(parts[:, i, 2, :], rest[:, i, :], parts[:, i, 1, :], ALU.subtract)\
                        .then_inc(lo_ready, 1)

            deviations(range(1))
            normalise_x(dve, nc.vector, 0)
            deviations(range(1, B))
            normalise_x(dve, nc.vector, 1)
            split_rest(0)
            split_lo(0)
            nc.vector.memset(o_bank[:, :], 0.0).then_inc(o_filled, 1)

            steps = [0]

            def step(ins):
                steps[0] += 1
                ins.then_inc(route_step, 1)
                dve.wait_ge(route_step, steps[0])

            def by_token(v):
                return v.rearrange("p (t o) -> p t o", o=1).to_broadcast([P, NT, E])

            def by_expert(v):
                return v.rearrange("p (o e) -> p o e", o=1).to_broadcast([P, NT, E])

            def choose_experts():
                dve.wait_ge(consts_ready, 2)
                for i in (VB - 2, VB - 1):
                    wait_free(dve, f"v{i}")
                step(nc.vector.tensor_reduce(rtc[:, 0, :], lg[:, :, :], AX.X, ALU.max))
                nc.vector.tensor_tensor(rt[:, 0], lg[:, :, :], by_token(rtc[:, 0, :]), ALU.subtract)\
                    .then_inc(gate_shift_ready, 1)
                step(nc.vector.tensor_tensor(rt[:, 2], lg[:, :, :], by_token(rtc[:, 0, :]), ALU.is_equal))
                step(nc.vector.scalar_tensor_tensor(out=lg[:, :, :], in0=rt[:, 2], scalar=-float(E), in1=by_expert(ev[:, :]),
                                                    op0=ALU.mult, op1=ALU.add))
                step(nc.vector.tensor_reduce(rtc[:, 1, :], lg[:, :, :], AX.X, ALU.min))
                step(nc.vector.tensor_scalar(rtc[:, 3, :], rtc[:, 1, :], float(E), None, ALU.add))
                nc.vector.tensor_tensor(onehot[:, :, :], by_expert(ev[:, :]), by_token(rtc[:, 3, :]), ALU.is_equal)\
                    .then_inc(onehot_ready, 1)

            def number_slots():
                dve.wait_ge(gate_exp_ready, 1)
                step(nc.vector.tensor_reduce(rtc[:, 4, :], rt[:, 1], AX.X, ALU.add))
                nc.vector.reciprocal(rtc[:, 2, :], rtc[:, 4, :]).then_inc(prob_ready, 1)
                dve.wait_ge(onehot_ready, 1)
                m = wait_full(dve, "route")
                nc.vector.tensor_tensor(rt[:, 2], m[:, 0:NT * E].rearrange("p (t e) -> p t e", e=E), onehot[:, :, :],
                                        ALU.mult).then_inc(free("route"), 1)
                wait_free(dve, "route")
                step(nc.vector.tensor_reduce(rtc[:, 5, :], rt[:, 2], AX.X, ALU.add))
                step(nc.vector.tensor_scalar(rtc[:, 6, :], rtc[:, 5, :], float(CAP), DROPPED, ALU.is_ge, ALU.mult))
                step(nc.vector.scalar_tensor_tensor(out=rtc[:, 7, :], in0=rtc[:, 3, :], scalar=float(CAP),
                                                    in1=rtc[:, 5, :], op0=ALU.mult, op1=ALU.add))
                step(nc.vector.tensor_tensor(rtc[:, 5, :], rtc[:, 7, :], rtc[:, 6, :], ALU.add))
                nc.vector.tensor_scalar(idx[:, :], rtc[:, 5, :], float(E * CAP), None, ALU.add).then_inc(idx_ready, 1)
                dve.wait_ge(gains_loaded, 48)
                nc.vector.tensor_copy(inv_row[:, 0, :], row_i[:, :]).then_inc(cum_gain_step, 1)
                dve.wait_ge(cum_gain_step, 1)
                nc.vector.reciprocal(inv_row[:, 1, :], inv_row[:, 0, :]).then_inc(cum_gain_step, 1)
                dve.wait_ge(cum_gain_step, 2)
                nc.vector.tensor_tensor(cum_gain[:, :, :],
                                        inv_row[:, 1, :].rearrange("p (t o) -> p t o", o=1).to_broadcast([P, QT, H]),
                                        gains[:, 2, :].rearrange("p (o h) -> p o h", o=1).to_broadcast([P, QT, H]),
                                        ALU.mult).then_inc(cum_gain_step, 1)

            def row_maxima(k, i):
                n = k * S1N + i
                dve.wait_ge(s1_full, n + 1)
                blocks = query_blocks(0, i)
                w = (blocks[0][1] + 1) * P
                h0, qt = blocks[0]
                c = len(blocks)
                nc.vector.tensor_reduce(mx[:, k % 2, h0:h0 + c, qt], s1_bank[n % 2][:, 0:c * w].rearrange("p (c w) -> p c w", c=c),
                                        AX.X, ALU.max).then_inc(s1_free, 1)

            def normalise(k):
                b, g = divmod(k, NG)
                m = wait_full(dve, f"oT{k}")
                ov = m[:, :].rearrange("p (t j r) -> p t j r", t=QT, j=G)
                nc.vector.reciprocal(rec[:, :, :], ov[:, :, :, HD]).then_inc(norm_step, 1)
                dve.wait_ge(norm_step, 2 * k + 1)
                gain = gains[:, 0, g * G:(g + 1) * G].rearrange("p (o j) -> p o j", o=1).to_broadcast([P, QT, G])
                nc.vector.tensor_tensor(recg[:, :, :], rec[:, :, :], gain, ALU.mult).then_inc(norm_step, 1)
                dve.wait_ge(norm_step, 2 * k + 2)
                weight = recg[:, :, :].rearrange("p t (j o) -> p t j o", o=1).to_broadcast([P, QT, G, HD])
                nc.vector.tensor_tensor(onorm[:, :, :, :], ov[:, :, :, 0:HD], weight, ALU.mult).then_inc(free(f"oT{k}"), 1)
                wait_free(dve, f"oT{k}")
                if g == 0:
                    dve.wait_ge(base_ready, b + 1)
                av = attn[:, b * QT:(b + 1) * QT, g * G * HD:(g + 1) * G * HD].rearrange("p t (j d) -> p t j d", j=G)
                nc.vector.tensor_tensor(av, av, onorm[:, :, :, :], ALU.add).then_inc(attn_ready, 1)

            def take_off_means(b):
                m = wait_full(dve, f"cum{b}")
                gain = cum_gain[:, :, :].rearrange("p t h -> p (t h)").rearrange("p (n o) -> p n o", o=1).to_broadcast([P, QT * H, HD])
                if b == 0:
                    dve.wait_ge(cum_gain_step, 3)
                nc.vector.tensor_tensor(cum_part[:, :, :, :].rearrange("p t h d -> p (t h) d"),
                                        m[:, :].rearrange("p (n d) -> p n d", d=HD), gain, ALU.mult)\
                    .then_inc(free(f"cum{b}"), 1)
                wait_free(dve, f"cum{b}")
                dve.wait_ge(skip_ready, b + 1)
                av = attn[:, b * QT:(b + 1) * QT, :].rearrange("p t d -> p (t d)")
                nc.vector.tensor_tensor(av, av, cum_part[:, :, :, :].rearrange("p t h d -> p (t h d)"), ALU.subtract)\
                    .then_inc(base_ready, 1)

            def finish(b):
                m = wait_full(dve, f"proj{b}")
                dve.wait_ge(silu_ready, NT)
                if b >= 2:
                    dve.wait_ge(y_stored[b % 2], 16 * (b // 2))
                fv = fg[:, b * QT:(b + 1) * QT, :].rearrange("p t d -> p (t d)")
                nc.vector.tensor_tensor(y_sb[:, b % 2, :], m[:, :], fv, ALU.mult).then_inc(free(f"proj{b}"), 1)
                wait_free(dve, f"proj{b}")
                xv = x_sb[:, b * QT:(b + 1) * QT, :].rearrange("p t d -> p (t d)")
                nc.vector.tensor_tensor(y_sb[:, b % 2, :], y_sb[:, b % 2, :], xv, ALU.add).then_inc(y_ready, 1)

            def part(k, kind, arg):
                if kind == "s1":
                    row_maxima(k + LAG, arg)
                elif kind == "route_a":
                    choose_experts()
                elif kind == "route_b":
                    number_slots()
                elif kind == "qk":
                    split_rest(arg)
                elif kind == "qk_low":
                    split_lo(arg)
                elif kind == "res":
                    m = wait_full(dve, f"res{arg}")
                    nc.vector.tensor_copy(slot_xT[:, arg * CAP:(arg + 1) * CAP], m[:, 0:CAP]).then_inc(free(f"res{arg}"), 1)
                elif kind == "resT":
                    m = wait_full(dve, f"resT{arg}")
                    nc.vector.tensor_copy(slot_sb[:, 4 * arg:4 * arg + 4, :].rearrange("p k d -> p (k d)"), m[:, :])\
                        .then_inc(free(f"resT{arg}"), 1)
                elif kind == "oT":
                    normalise(arg)
                elif kind == "cum":
                    take_off_means(arg)
                elif kind == "maxT":
                    m = wait_full(dve, f"maxT{arg}")
                    dve.wait_ge(nm_hi_ready, arg + 1)
                    nc.vector.scalar_tensor_tensor(out=mrest[:, :], in0=m[0:G * QT, 0:P], scalar=-1.0,
                                                   in1=negm[:, arg % 2, 0, :], op0=ALU.mult, op1=ALU.subtract)\
                        .then_inc(free(f"maxT{arg}"), 1)
                elif kind == "max_low":
                    dve.wait_ge(nm_mid_ready, arg + 1)
                    nc.vector.tensor_tensor(negm[:, arg % 2, 2, :], mrest[:, :], negm[:, arg % 2, 1, :], ALU.subtract)\
                        .then_inc(nm_lo_ready, 1)
                elif kind == "proj":
                    finish(arg)

            for k in STAGES:
                for kind, arg in orders[k]:
                    part(k, kind, arg)
            normalise(K - 1)
            finish(B - 1)


_INS = ["L0_attn_x", "L0_attn_qk_w", "L0_attn_qk_b", "L0_attn_v_w", "L0_attn_cproj_w", "L0_attn_resid_gain",
        "L0_attn_skip_gain", "L0_attn_centre_gain", "L0_ffn_gate_w", "L0_ffn_w1", "L0_ffn_w2"]


def kernel(**inputs):
    import numpy as _np
    import concourse.bacc as _bacc
    from concourse import mybir as _mybir
    from concourse.bass_utils import run_bass_kernel_spmd as _run

    nc = _bacc.Bacc("TRN2", target_bir_lowering=False, num_devices=1)
    arrays, args = {}, []
    for name in _INS:
        a = _np.ascontiguousarray(inputs[name])
        arrays[f"in_{name}"] = a
        args.append(nc.dram_tensor(f"in_{name}", a.shape, _mybir.dt.from_np(a.dtype), kind="ExternalInput").ap())
    shape = inputs["L0_attn_x"].shape
    args.append(nc.dram_tensor("out_0", shape, _mybir.dt.float32, kind="ExternalOutput").ap())
    attention_moe_block(nc, *args)
    r = _run(nc, [arrays], core_ids=[0])
    return r.results[0]["out_0"]
```

```python
from contextlib import ExitStack

import numpy as np

import concourse.bass as bass
from concourse import mybir

F32 = mybir.dt.float32
BF16 = mybir.dt.bfloat16
I32 = mybir.dt.int32
U32 = mybir.dt.uint32
ALU = mybir.AluOpType
ACT = mybir.ActivationFunctionType
AX = mybir.AxisListType

P = 128
NEG = -1.0e30
ONE_ONE = float(np.array([0x3F803F80], np.uint32).view(np.float32)[0])
DROPPED = 1.0e6


def attention_moe_block(nc, x, qk_w, qk_b, v_w, cproj_w, resid_gain, skip_gain, centre_gain, gate_w, w1, w2, out):
    B, S, D = x.shape
    H = resid_gain.shape[1]
    HD = D // H
    E, _, F = w1.shape
    T = B * S
    CAP = int(1.25 * T / E)
    NT = T // P
    QT = S // P
    G = 4
    NG = H // G
    FC = F // P
    SLOTS = E * CAP
    SB = SLOTS // P
    PAIRS = 6
    R = PAIRS * HD
    MR = R + 3
    S1N = 2 * G + G // 2 + 1
    FUSED = 2 * G
    S2N = 2 * G + G // 2
    VB = (NT + 2) // 3
    WR = 3
    PART_PAIRS = ((0, 0), (0, 1), (1, 0), (1, 1), (0, 2), (2, 0))
    SCALE = float(HD) ** -0.5
    assert D == P and S == 4 * P and HD == 8 and H == 16 and SLOTS % P == 0

    K = B * NG
    LAG = 2
    STAGES = range(-LAG, K)
    V_AHEAD = 1
    V_AT = 1
    ROUTE_A, ROUTE_B = 6, 9
    SCATTER_AT, SCATTER_EVERY = 9, 1
    QK1_AT = 7
    QK_AT = 7
    QK_APART, LOW_APART = 0, 0
    PLACE_APART, PLACE_WAIT = 4, 3
    MAX_AT, MAX_APART = 2, 1
    WEIGH_AT = (0, 2, 4, 5)
    COPY_AT, TURN_AT = 6, 8
    LAST_WEIGH_AT = (0, 1, 2, 3)
    LAST_COPY_AT, LAST_TURN_AT = 4, 5
    FINAL_AT = (10, 10, 10, 10)
    CUM_AT = 9
    SLOTS_AT = 1 * S1N + 4
    SLOTS_TURN = 2 * S1N + 5
    FFN_AT = 3 * S1N
    FFN_EVERY = 3.7
    RES_APART = 3
    RES_TURN = 8 * S1N + 5
    CLEAR_AT = 2 * S1N + 9
    SILU_AT = 13
    SILU_STEP, PAUSE = 0, 5
    GATHER_AT, GATHER_EVERY = 100, 2
    GATE_AT, GATE_EVERY = 136, 1
    PREFIX0_AT = 7
    PREFIX_AT = 0 * S1N + 10
    FIRST_TURN, FIRST_PROJ = 7, 9
    ATT_TURN, ATT_PROJ = 2, 7
    tasks = {}

    def place(kind, arg, step):
        tasks.setdefault(step, []).append((kind, arg))

    start = -LAG * S1N
    for i in range(V_AHEAD, VB):
        place("v", i, start + V_AT + i - V_AHEAD)
    place("prefix", 0, start + PREFIX0_AT)
    place("route_a", 0, start + ROUTE_A)
    place("route_b", 0, start + ROUTE_B)
    for t in range(NT):
        place("scatter", t, start + SCATTER_AT + t * SCATTER_EVERY)
    for b in range(1, B):
        at = QK1_AT if b == 1 else ((b - 1) * NG - 1) * S1N + QK_AT
        place("qk", (b, 0), at)
        place("qk", (b, 1), at + QK_APART)
        place("qk_low", b, at + QK_APART + LOW_APART)
        place("place", b, at + QK_APART + PLACE_APART if b == 1 else (b - 1) * NG * S1N + PLACE_WAIT)
        place("prefix", b, (b - 1) * NG * S1N + PREFIX_AT)
    for k in range(K):
        place("maxT", k, (k - 1) * S1N + MAX_AT)
        place("max_low", k, (k - 1) * S1N + MAX_AT + MAX_APART)
    for k in range(K - 1):
        last = k == K - 2
        at = (k + 1) * S1N
        for kb, step in enumerate(LAST_WEIGH_AT if last else WEIGH_AT):
            place("weigh", (k, kb), at + step)
        place("copy_o", k, at + (LAST_COPY_AT if last else COPY_AT))
        place("oT", k, at + (LAST_TURN_AT if last else TURN_AT))
    for kb, step in zip((0, 1, 3, 2), FINAL_AT):
        place("weigh", (K - 1, kb), (K - 1) * S1N + step)
    place("copy_o", K - 1, K * S1N - 1)
    for b in range(B):
        place("cum", b, b * NG * S1N + CUM_AT)
    place("slots_load", 0, SLOTS_AT)
    for i in range(SB // 4):
        place("slotT", i, SLOTS_TURN + i)
    for e in range(E):
        at = FFN_AT + int(e * FFN_EVERY)
        place("hid", (e, 0), at)
        place("hid", (e, 1), at + 1)
        place("res", e, at + RES_APART)
    for i in range(SB // 4):
        place("resT", i, RES_TURN + i)
    place("clear", 0, CLEAR_AT)
    for t in range(NT):
        place("gather", t, GATHER_AT + int(t * GATHER_EVERY))
    for b in range(B):
        place("gate", b, GATE_AT + b * GATE_EVERY)
    for b in range(1, B - 1):
        place("attT", b, (SILU_AT + b) * S1N + ATT_TURN)
        place("proj", b, (SILU_AT + b) * S1N + ATT_PROJ)
    place("attT", 0, SILU_AT * S1N + FIRST_TURN)
    place("proj", 0, SILU_AT * S1N + FIRST_PROJ)

    def stage_order(k):
        order, banks = [], list(range(S2N)) if k >= 0 else []
        for i in range(S1N):
            pause = k == SILU_AT and SILU_STEP < i <= SILU_STEP + PAUSE
            behind = len(banks) > S2N - i
            for _ in range(0 if pause else 2 if behind else 1):
                if banks:
                    order.append(("s2", banks.pop(0)))
            if k + LAG < K:
                order.append(("s1", i))
            order += tasks.get(k * S1N + i, ())
            if (k, i) == (SILU_AT, SILU_STEP):
                order.append(("silu", 0))
        return order + [("s2", i) for i in banks]

    orders = {k: stage_order(k) for k in STAGES}

    uses = ["columns", "xT0", "q0", "k0"] + [f"xT{b}" for b in range(1, B)] + [f"v{i}" for i in range(V_AHEAD)]
    for k in STAGES:
        for kind, arg in orders[k]:
            if kind == "qk":
                uses.append(f"{'qk'[arg[1]]}{arg[0]}")
            elif kind == "hid":
                uses.append(f"hid{arg[0]}_{arg[1]}")
            elif kind == "route_b":
                uses.append("route")
            elif kind in ("v", "maxT", "slotT", "res", "resT", "oT", "cum", "attT", "proj"):
                uses.append(f"{kind}{arg}")
    uses += [f"oT{K - 1}", f"attT{B - 1}", f"proj{B - 1}"]
    use_of = {name: n for n, name in enumerate(uses)}

    with ExitStack() as ctx:
        def sb(name, shape, dt=F32):
            return ctx.enter_context(nc.sbuf_tensor(name, shape, dt))

        def sem(name):
            return ctx.enter_context(nc.semaphore(name))

        def dram(name, shape, dt):
            return nc.dram_tensor(name, shape, dt, kind="Internal").ap()

        max_rows = dram("max_rows", [K, 3, G, S], BF16)
        slot_rows = dram("slot_rows", [SLOTS, D], F32)
        result_rows = dram("result_rows", [SLOTS, D], F32)

        stack = sb("stack", [P, 2, H, 2, S], BF16)
        qs, ks = stack[:, :, :, 0, :], stack[:, :, :, 1, :]
        probs = sb("probs", [P, 2, S2N, S])
        x_sb = sb("x_sb", [P, NT, D])
        xn = sb("xn", [P, NT, D])
        fg = xn
        slot_xT = sb("slot_xT", [P, SLOTS])
        slot_sb = sb("slot_sb", [P, SB, D])
        v_aug = sb("v_aug", [P, NT, H, HD + 1])
        v_pre = sb("v_pre", [P, 2, D])
        w1_sb = sb("w1_sb", [P, WR, F])
        w2_sb = sb("w2_sb", [P, WR, FC, D])
        hid = sb("hid", [P, 2, FC, CAP])
        parts = sb("parts", [P, 2, 3, S], BF16)
        rest = sb("rest", [P, 2, S])
        attn = sb("attn", [P, NT, D])
        xnT = [slot_xT[:, b * S:(b + 1) * S] for b in range(2)]
        xnT += [attn[:, b * QT:(b + 1) * QT, :].rearrange("p t d -> p (t d)") for b in range(2, B)]
        warm = sb("warm", [P, 1])
        oT_sb = sb("oT_sb", [P, 2, S])
        att_T = sb("att_T", [P, S])
        y_sb = rest
        wqk = sb("wqk", [P, 2, HD, H])
        wqk_raw = att_T[:, 0:2 * D]
        brow_raw = att_T[0:1, 2 * D:4 * D]
        wvg = sb("wvg", [P, D + E])
        wc = sb("wc", [P, D])
        gate_sb = sb("gate_sb", [E, D])
        brow = sb("brow", [1, 2, HD, H])
        bias = sb("bias", [P, 2])
        gains = sb("gains", [P, 3, H])
        identf = sb("identf", [P, P])
        identb = sb("identb", [P, P], BF16)
        causal = sb("causal", [P, S], BF16)
        maskneg = causal[:, S - P:S]
        before = sb("before", [P, P], BF16)
        onesb = sb("onesb", [P, P], BF16)
        upto = sb("upto", [P, P])
        onesf = sb("onesf", [P, P])
        stats = sb("stats", [P, NT, 6])
        mv = sb("mv", [P, NT, 2])
        rstd = sb("rstd", [P, 4, NT])
        lg = sb("lg", [P, NT, E])
        rt = oT_sb[:, :, :].rearrange("p a t -> p (a t)")[:, 0:3 * NT * E].rearrange("p (a t e) -> p a t e", a=3, t=NT)
        rtc = sb("rtc", [P, 8, NT])
        onehot = sb("onehot", [P, NT, E], BF16)
        ev = sb("ev", [P, E])
        idx = sb("idx", [P, NT], I32)
        row_i = sb("row_i", [P, QT], I32)
        inv_row = sb("inv_row", [P, 2, QT])
        mx = sb("mx", [P, 2, G, QT])
        negm = sb("negm", [G * QT, 2, 3, P], BF16)
        mrest = sb("mrest", [G * QT, P])
        rec = sb("rec", [P, QT, G])
        recg = sb("recg", [P, QT, G])
        onorm = sb("onorm", [P, QT, G, HD])
        cum_gain = sb("cum_gain", [P, QT, H])
        cum_part = sb("cum_part", [P, QT, H, HD])

        def bank(name):
            return ctx.enter_context(nc.psum_tensor(name, [P, 512], F32))

        s1_bank = [bank(f"s1_bank{i}") for i in range(2)]
        s2_bank = [bank(f"s2_bank{i}") for i in range(3)]
        o_bank = bank("o_bank")
        mi_bank = [bank(f"mi_bank{i}") for i in range(2)]

        x_loaded = [sem(f"x_loaded{b}") for b in range(B)]
        small_loaded = sem("small_loaded")
        wqk_loaded = sem("wqk_loaded")
        wv_loaded = sem("wv_loaded")
        brow_turned = sem("brow_turned")
        wqk_turned = sem("wqk_turned")
        wc_loaded = sem("wc_loaded")
        gains_loaded = sem("gains_loaded")
        const_step = sem("const_step")
        consts_ready = sem("consts_ready")
        q_filled = [sem(f"q_filled{i}") for i in range(2)]
        k_filled = sem("k_filled")
        slots_filled = sem("slots_filled")
        o_filled = sem("o_filled")
        ones_filled = sem("ones_filled")
        ln_step = sem("ln_step")
        var_ready = sem("var_ready")
        std_ready = sem("std_ready")
        rstd_ready = sem("rstd_ready")
        xn_ready = [sem(f"xn_ready{b}") for b in range(B)]
        mi_full = [sem(f"mi_full{i}") for i in range(2)]
        mi_free = [sem(f"mi_free{i}") for i in range(2)]
        wvg_ready = sem("wvg_ready")
        hi_ready = sem("hi_ready")
        mid_ready = sem("mid_ready")
        lo_ready = sem("lo_ready")
        parts_placed = [sem(f"parts_placed{b}") for b in range(B)]
        v_ready = sem("v_ready")
        vpre_ready = sem("vpre_ready")
        route_step = sem("route_step")
        onehot_ready = sem("onehot_ready")
        gate_shift_ready = sem("gate_shift_ready")
        gate_exp_ready = sem("gate_exp_ready")
        prob_ready = sem("prob_ready")
        idx_ready = sem("idx_ready")
        slots_cleared = sem("slots_cleared")
        scattered = sem("scattered")
        slots_loaded = sem("slots_loaded")
        w_ring = [sem(f"w_ring{i}") for i in range(WR)]
        results_stored = sem("results_stored")
        fg_cleared = sem("fg_cleared")
        gathered = [sem(f"gathered{b}") for b in range(B)]
        silu_ready = sem("silu_ready")
        s1_full = sem("s1_full")
        s1_free = sem("s1_free")
        s2_full = sem("s2_full")
        s2_free = sem("s2_free")
        masked = sem("masked")
        weighed = sem("weighed")
        o_copied = sem("o_copied")
        nm_hi_ready = sem("nm_hi_ready")
        nm_mid_ready = sem("nm_mid_ready")
        nm_lo_ready = sem("nm_lo_ready")
        max_stored = [sem(f"max_stored{i}") for i in range(2)]
        max_placed = [sem(f"max_placed{i}") for i in range(2)]
        cum_gain_step = sem("cum_gain_step")
        skip_ready = sem("skip_ready")
        base_ready = sem("base_ready")
        norm_step = sem("norm_step")
        attn_ready = sem("attn_ready")
        gated = sem("gated")
        y_ready = sem("y_ready")
        y_stored = [sem(f"y_stored{i}") for i in range(2)]

        def take(name):
            n = use_of[name]
            if n >= 2:
                nc.tensor.wait_ge(mi_free[n % 2], n // 2)
            return mi_bank[n % 2]

        def full(name):
            return mi_full[use_of[name] % 2]

        def free(name):
            return mi_free[use_of[name] % 2]

        def wait_full(eng, name):
            eng.wait_ge(full(name), use_of[name] // 2 + 1)
            return mi_bank[use_of[name] % 2]

        def wait_free(eng, name):
            eng.wait_ge(free(name), use_of[name] // 2 + 1)

        def wait_x_turned(eng, b):
            wait_free(eng, f"xT{b}")

        def placed_dmas(b):
            return PAIRS + (1 if b >= 2 else 0)

        def query_blocks(g, i):
            if i < 2 * G:
                return [(g * G + i % G, QT - 1 - i // G)]
            if i < S1N - 1:
                return [(g * G + 2 * (i - 2 * G) + j, 1) for j in range(2)]
            return [(g * G + j, 0) for j in range(G)]

        def copy_out(eng, out, src):
            if eng is nc.vector:
                return nc.vector.tensor_copy(out, src)
            return nc.scalar.activation(out, src, ACT.Copy)

        def copy_o(eng, k):
            eng.wait_ge(weighed, k + 1)
            if k >= 2:
                wait_full(eng, f"oT{k - 2}")
            copy_out(eng, oT_sb[:, k % 2, :], o_bank[:, :]).then_inc(o_copied, 1)

        def copy_attT(eng, b):
            m = wait_full(eng, f"attT{b}")
            copy_out(eng, att_T[:, :], m[:, :]).then_inc(free(f"attT{b}"), 1)

        def split_lo(eng, engine, b):
            for i in range(2):
                eng.wait_ge(mid_ready, 2 * b + i + 1)
                engine.tensor_tensor(parts[:, i, 2, :], rest[:, i, :], parts[:, i, 1, :], ALU.subtract)\
                    .then_inc(lo_ready, 1)

        block = ctx.enter_context(nc.Block())

        @block.sync
        def _(sp):
            for b in range(B):
                sp.dma_start(x_sb[:, b * QT:(b + 1) * QT, :], x[b].rearrange("(t p) d -> p t d", p=P))\
                    .then_inc(x_loaded[b], 16)
            sp.dma_start(wvg[:, 0:D], v_w).then_inc(wv_loaded, 16)
            sp.dma_start(wc[:, :], cproj_w).then_inc(wc_loaded, 16)
            for i, gain in enumerate((resid_gain, skip_gain, centre_gain)):
                sp.dma_start(gains[:, i, :], gain.rearrange("a h b c -> (a b c) h").to_broadcast([P, H]))\
                    .then_inc(gains_loaded, 16)

            by_part = parts[:, :, :, :].rearrange("p i c t -> p (i c) t")

            def place_parts(b):
                par = b % 2
                if b >= 2:
                    sp.wait_ge(s2_full, (b - 1) * NG * S2N)
                    sp.dma_start(qs[R:MR, par], qs[64:64 + MR - R, par]).then_inc(parts_placed[b], 16)
                else:
                    sp.wait_ge(q_filled[b], 1)
                    sp.wait_ge(k_filled, b + 1)
                for row, (cq, ck) in enumerate(PART_PAIRS):
                    if row == 0:
                        sp.wait_ge(hi_ready, 2 * b + 2)
                    elif row == 1:
                        sp.wait_ge(mid_ready, 2 * b + 2)
                    elif row == 4:
                        sp.wait_ge(lo_ready, 2 * b + 2)
                    rows = slice(row * HD, (row + 1) * HD)
                    sp.dma_start(stack[rows, par], by_part[:, cq:4 + ck:3 + ck - cq, :]).then_inc(parts_placed[b], 16)

            def load_expert(e):
                if e >= WR:
                    wait_full(sp, f"res{e - WR}")
                sp.dma_start(w1_sb[:, e % WR, :], w1[e]).then_inc(w_ring[e % WR], 16)
                sp.dma_start(w2_sb[:, e % WR], w2[e].rearrange("(c p) d -> p c d", p=P)).then_inc(w_ring[e % WR], 16)

            def place_max(k):
                sp.wait_ge(nm_lo_ready, k + 1)
                b, g = divmod(k, NG)
                sp.dma_start(max_rows[k].rearrange("c h (t q) -> (h t) c q", q=P), negm[:, k % 2]).then_inc(max_stored[k % 2], 16)
                sp.wait_ge(max_stored[k % 2], 16 * (k // 2 + 1))
                sp.dma_start(stack[R:MR, b % 2, g * G:(g + 1) * G, 0, :], max_rows[k]).then_inc(max_placed[k % 2], 16)

            def store_y(b):
                sp.wait_ge(y_ready, b + 1)
                sp.dma_start(out[b].rearrange("(t p) d -> p t d", p=P),
                             y_sb[:, b % 2, :].rearrange("p (t d) -> p t d", t=QT)).then_inc(y_stored[b % 2], 16)

            place_parts(0)
            sp.wait_ge(slots_filled, 1)
            sp.dma_start(slot_rows.rearrange("(k p) d -> p k d", p=P), slot_sb[:, :, :]).then_inc(slots_cleared, 16)
            for e in range(WR):
                load_expert(e)
            for k in STAGES:
                for kind, arg in orders[k]:
                    if kind == "max_low":
                        place_max(arg)
                    elif kind == "place":
                        place_parts(arg)
                    elif kind == "slots_load":
                        sp.wait_ge(scattered, 16 * NT)
                        sp.dma_start(slot_sb[:, :, :], slot_rows.rearrange("(k p) d -> p k d", p=P))\
                            .then_inc(slots_loaded, 16)
                    elif kind == "res" and arg + WR < E:
                        load_expert(arg + WR)
                    elif kind == "resT" and arg == SB // 4 - 1:
                        for i in range(SB // 4):
                            wait_free(sp, f"resT{i}")
                        sp.dma_start(result_rows.rearrange("(k p) d -> p k d", p=P), slot_sb[:, :, :])\
                            .then_inc(results_stored, 16)
                    elif kind == "proj":
                        store_y(arg)
            store_y(B - 1)
            for i in range(2):
                sp.wait_ge(y_stored[i], 16 * (B // 2))

        @block.gpsimd
        def _(pool):
            nc.gpsimd.memset(identf[:, :], 0.0).then_inc(const_step, 1)
            nc.gpsimd.memset(onesf[:, :], 1.0).then_inc(const_step, 1)
            nc.gpsimd.memset(onesb[:, :], 1.0).then_inc(const_step, 1)
            nc.gpsimd.memset(causal[:, :], 0.0).then_inc(const_step, 1)
            pool.wait_ge(const_step, 4)
            nc.gpsimd.affine_select(out=identf[:, :], in_=identf[:, :], compare_op=ALU.not_equal, fill=1.0,
                                    base=0, pattern=[[-1, P]], channel_multiplier=1).then_inc(const_step, 1)
            nc.gpsimd.affine_select(out=maskneg, in_=maskneg, compare_op=ALU.is_ge, fill=NEG,
                                    base=0, pattern=[[-1, P]], channel_multiplier=1)
            pool.wait_ge(const_step, 5)
            nc.gpsimd.tensor_copy(identb[:, :], identf[:, :]).then_inc(consts_ready, 1)
            nc.gpsimd.memset(ks[:, 0].bitcast(F32), ONE_ONE).then_inc(k_filled, 1)
            nc.gpsimd.memset(qs[:, 0].bitcast(F32), 0.0).then_inc(q_filled[0], 1)
            nc.gpsimd.affine_select(out=before[:, :], in_=onesb[:, :], compare_op=ALU.is_gt, fill=0.0,
                                    base=0, pattern=[[1, P]], channel_multiplier=-1)
            nc.gpsimd.affine_select(out=upto[:, :], in_=onesf[:, :], compare_op=ALU.is_ge, fill=0.0,
                                    base=0, pattern=[[1, P]], channel_multiplier=-1)
            nc.gpsimd.iota(ev[:, :], [[1, E]], base=-E, channel_multiplier=0,
                           allow_small_or_imprecise_dtypes=True)
            nc.gpsimd.iota(row_i[:, :], [[P, QT]], base=1, channel_multiplier=1).then_inc(consts_ready, 1)
            nc.gpsimd.memset(v_aug[:, :, :, HD:HD + 1], 1.0).then_inc(ones_filled, 1)
            nc.gpsimd.memset(slot_sb[:, :, :], 0.0).then_inc(slots_filled, 1)
            nc.gpsimd.memset(qs[:, 1].bitcast(F32), 0.0).then_inc(q_filled[1], 1)
            nc.gpsimd.memset(ks[:, 1].bitcast(F32), ONE_ONE).then_inc(k_filled, 1)

            def scatter(t):
                if t == 0:
                    pool.wait_ge(idx_ready, 1)
                    pool.wait_ge(slots_cleared, 16)
                pool.indirect_dma_start(
                    slot_rows, bass.IndirectOffsetOnAxis(ap=idx[:, t:t + 1].bitcast(U32), axis=0),
                    xn[:, t, :], None, bounds_check=SLOTS - 1, oob_is_err=False).then_inc(scattered, 16)

            def gather(t):
                if t == 0:
                    pool.wait_ge(fg_cleared, 1)
                    pool.wait_ge(results_stored, 16)
                pool.indirect_dma_start(
                    fg[:, t, :], None, result_rows,
                    bass.IndirectOffsetOnAxis(ap=idx[:, t:t + 1].bitcast(U32), axis=0),
                    bounds_check=SLOTS - 1, oob_is_err=False).then_inc(gathered[t // QT], 16)

            def prefix_values(b):
                if b == 0:
                    pool.wait_ge(v_ready, VB)
                    pool.wait_ge(gains_loaded, 48)
                else:
                    wait_full(pool, f"cum{b - 1}")
                    if b >= 2:
                        wait_full(pool, f"k{b}")
                va = v_aug[:, b * QT:(b + 1) * QT, :, 0:HD]
                pre = v_pre[:, :, :].rearrange("p t (h d) -> p t h d", h=H)
                nc.gpsimd.tensor_tensor(pre[:, 0], va[:, 0], va[:, 1], ALU.add).then_inc(vpre_ready, 1)
                pool.wait_ge(vpre_ready, 2 * b + 1)
                nc.gpsimd.tensor_tensor(pre[:, 1], pre[:, 0], va[:, 2], ALU.add).then_inc(vpre_ready, 1)
                for t in range(QT):
                    ins = nc.gpsimd.tensor_tensor(
                        attn[:, b * QT + t, :].rearrange("p (h d) -> p h d", h=H), va[:, t],
                        gains[:, 1, :].rearrange("p (h o) -> p h o", o=1).to_broadcast([P, H, HD]), ALU.mult)
                ins.then_inc(skip_ready, 1)

            def mask_probs(k, bank):
                blocks = probs[:, k % 2, :, :].rearrange("p u (c q) -> p (u c) q", q=P)
                for n, first, apart in ((G, 0, QT), (2 * G, G * QT, QT), (2 * G, G * QT + 3, QT), (S2N, 2 * G * QT, 2)):
                    if n == bank + 1:
                        pool.wait_ge(s2_free, k * S2N + n)
                        v = blocks[:, first:first + apart * (G - 1) + 1:apart, :]
                        nc.gpsimd.affine_select(out=v, in_=v, compare_op=ALU.is_ge, fill=0.0, base=0,
                                                pattern=[[0, G], [1, P]], channel_multiplier=-1).then_inc(masked, 1)

            def gate(b):
                pool.wait_ge(gathered[b], 16 * QT)
                if b == 0:
                    pool.wait_ge(prob_ready, 1)
                v = fg[:, b * QT:(b + 1) * QT, :]
                weight = rtc[:, 2, b * QT:(b + 1) * QT].rearrange("p (t o) -> p t o", o=1).to_broadcast([P, QT, D])
                nc.gpsimd.tensor_tensor(v, v, weight, ALU.mult).then_inc(gated, 1)

            for k in STAGES:
                for kind, arg in orders[k]:
                    if kind == "s2":
                        mask_probs(k, arg)
                    elif kind == "qk_low":
                        split_lo(pool, nc.gpsimd, arg)
                    elif kind == "prefix":
                        prefix_values(arg)
                    elif kind == "scatter":
                        scatter(arg)
                    elif kind == "clear":
                        pool.wait_ge(scattered, 16 * NT)
                        nc.gpsimd.memset(fg[:, :, :], 0.0).then_inc(fg_cleared, 1)
                    elif kind == "gather":
                        gather(arg)
                    elif kind == "gate":
                        gate(arg)

        @block.scalar
        def _(act):
            act.dma_start(wqk_raw, qk_w).then_inc(wqk_loaded, 16)
            act.dma_start(gate_sb[:, :], gate_w).then_inc(small_loaded, 16)
            act.dma_start(brow_raw, qk_b.rearrange("(o n) -> o n", o=1)).then_inc(small_loaded, 16)
            act.wait_ge(const_step, 4)
            nc.scalar.activation(warm[:, :], onesf[:, 0:1], ACT.Sqrt)
            act.wait_ge(small_loaded, 32)
            nc.scalar.activation(brow[:, :, :, :], brow_raw.rearrange("o (i h d) -> o i d h", i=2, h=H), ACT.Copy)\
                .then_inc(brow_turned, 1)
            act.wait_ge(wqk_loaded, 16)
            nc.scalar.activation(wqk[:, :, :, :], wqk_raw.rearrange("p (i h d) -> p i d h", i=2, h=H), ACT.Copy)\
                .then_inc(wqk_turned, 1)

            def deviation(turn):
                act.wait_ge(var_ready, turn + 1)
                ts = slice(turn * QT, NT if turn else QT)
                nc.scalar.activation(rstd[:, 1, ts], rstd[:, 0, ts], ACT.Sqrt).then_inc(std_ready, 1)

            def copy_xT(b):
                m = wait_full(act, f"xT{b}")
                nc.scalar.activation(xnT[b], m[:, :], ACT.Copy).then_inc(free(f"xT{b}"), 1)

            def split_hi(b, i):
                if b and i == 0:
                    act.wait_ge(parts_placed[b - 1], 16 * placed_dmas(b - 1))
                elif b == 0:
                    wait_free(act, "columns")
                m = wait_full(act, f"{'qk'[i]}{b}")
                nc.scalar.activation(parts[:, i, 0, :], m[:, :], ACT.Identity,
                                     bias=bias[:, i:i + 1]).then_inc(hi_ready, 1)

            def split_mid(b):
                for i, n in enumerate("qk"):
                    wait_free(act, f"{n}{b}")
                    nc.scalar.activation(parts[:, i, 1, :], rest[:, i, :], ACT.Copy).then_inc(mid_ready, 1)

            deviation(0)
            m = wait_full(act, "columns")
            nc.scalar.activation(wvg[:, D:D + E], m[:, 0:E], ACT.Copy).then_inc(wvg_ready, 1)
            nc.scalar.activation(bias[:, :], m[:, E:E + 2], ACT.Copy).then_inc(free("columns"), 1)
            copy_xT(0)
            deviation(1)
            for i in range(2):
                split_hi(0, i)
            split_mid(0)
            for b in range(1, B):
                copy_xT(b)
            act.wait_ge(ones_filled, 1)

            def copy_values(i):
                m = wait_full(act, f"v{i}")
                n = min(3, NT - 3 * i)
                vg = m[:, 0:n * (D + E)].rearrange("p (t c) -> p t c", t=n)
                nc.scalar.activation(v_aug[:, 3 * i:3 * i + n, :, 0:HD],
                                     vg[:, :, 0:D].rearrange("p t (h d) -> p t h d", h=H), ACT.Copy).then_inc(v_ready, 1)
                nc.scalar.activation(lg[:, 3 * i:3 * i + n, :], vg[:, :, D:D + E], ACT.Copy).then_inc(free(f"v{i}"), 1)

            for i in range(V_AHEAD):
                copy_values(i)

            def exponential(k, i):
                n = k * S2N + i
                if i == 0 and k >= 2:
                    act.wait_ge(weighed, k - 1)
                act.wait_ge(s2_full, n + 1)
                nc.scalar.activation(probs[:, k % 2, i, :], s2_bank[n % 3][:, :], ACT.Exp,
                                     scale=SCALE).then_inc(s2_free, 1)

            def part(k, kind, arg):
                if kind == "s2":
                    exponential(k, arg)
                elif kind == "v":
                    copy_values(arg)
                elif kind == "route_a":
                    act.wait_ge(gate_shift_ready, 1)
                    nc.scalar.activation(rt[:, 1], rt[:, 0], ACT.Exp).then_inc(gate_exp_ready, 1)
                elif kind == "qk":
                    split_hi(*arg)
                elif kind == "qk_low":
                    split_mid(arg)
                elif kind == "slotT":
                    m = wait_full(act, f"slotT{arg}")
                    nc.scalar.activation(slot_xT[:, arg * 4 * P:(arg + 1) * 4 * P], m[:, :], ACT.Copy)\
                        .then_inc(free(f"slotT{arg}"), 1)
                elif kind == "hid":
                    e, c = arg
                    m = wait_full(act, f"hid{e}_{c}")
                    nc.scalar.activation(hid[:, e % 2, 2 * c:2 * c + 2, :],
                                         m[:, 0:2 * CAP].rearrange("p (c s) -> p c s", c=2), ACT.Relu)\
                        .then_inc(free(f"hid{e}_{c}"), 1)
                elif kind == "copy_o" and k + LAG < K:
                    copy_o(act, arg)
                elif kind == "maxT":
                    m = wait_full(act, f"maxT{arg}")
                    if arg >= 2:
                        act.wait_ge(max_stored[arg % 2], 16 * (arg // 2))
                    nc.scalar.activation(negm[:, arg % 2, 0, :], m[0:G * QT, 0:P], ACT.Copy, scale=-1.0)\
                        .then_inc(nm_hi_ready, 1)
                elif kind == "max_low":
                    wait_free(act, f"maxT{arg}")
                    nc.scalar.activation(negm[:, arg % 2, 1, :], mrest[:, :], ACT.Copy).then_inc(nm_mid_ready, 1)
                elif kind == "silu":
                    for b in range(B):
                        act.wait_ge(gated, b + 1)
                        nc.scalar.activation(fg[:, b * QT:(b + 1) * QT, :], fg[:, b * QT:(b + 1) * QT, :], ACT.Silu)\
                            .then_inc(silu_ready, 1)
                elif kind == "attT" and k + LAG < K:
                    copy_attT(act, arg)

            for k in STAGES:
                for kind, arg in orders[k]:
                    part(k, kind, arg)

        @block.tensor
        def _(pe):
            pe.wait_ge(consts_ready, 1)
            pe.wait_ge(small_loaded, 32)
            m = take("columns")
            nc.tensor.transpose(m[:, 0:E], gate_sb[:, :], identf[0:E, 0:E])
            pe.wait_ge(brow_turned, 1)
            for i in range(2):
                col = brow[:, i].rearrange("o d h -> o (d h)")
                mm = nc.tensor.matmul(m[:, E + i:E + i + 1], col, identf[0:1, 0:1], start=True, stop=True,
                                      skip_group_check=True)
            mm.then_inc(full("columns"), 1)

            def turn_x(b):
                pe.wait_ge(xn_ready[b], 1)
                m = take(f"xT{b}")
                for t in range(QT):
                    mm = nc.tensor.transpose(m[:, t * P:(t + 1) * P], xn[:, b * QT + t, :], identf[:, :])
                mm.then_inc(full(f"xT{b}"), 1)

            def project_qk(b, i):
                m = take(f"{'qk'[i]}{b}")
                wait_x_turned(pe, b)
                w = wqk[:, i].rearrange("p d h -> p (d h)")
                nc.tensor.matmul(m[:, :], w, xnT[b], start=True, stop=True).then_inc(full(f"{'qk'[i]}{b}"), 1)

            turn_x(0)
            pe.wait_ge(wqk_turned, 1)
            for i in range(2):
                project_qk(0, i)
            for b in range(1, B):
                turn_x(b)

            def project_v(i):
                m = take(f"v{i}")
                if i == 0:
                    pe.wait_ge(wv_loaded, 16)
                    pe.wait_ge(wvg_ready, 1)
                for j in range(min(3, NT - 3 * i)):
                    t = 3 * i + j
                    if t % QT == 0:
                        wait_x_turned(pe, t // QT)
                    mm = nc.tensor.matmul(m[:, j * (D + E):(j + 1) * (D + E)],
                                          xnT[t // QT][:, t % QT * P:(t % QT + 1) * P], wvg[:, :],
                                          start=True, stop=True, skip_group_check=True)
                mm.then_inc(full(f"v{i}"), 1)

            for i in range(V_AHEAD):
                project_v(i)

            def count_ahead():
                pe.wait_ge(consts_ready, 2)
                pe.wait_ge(onehot_ready, 1)
                m = take("route")
                nc.tensor.matmul(m[:, 0:NT * E], before[:, :], onehot[:, :, :].rearrange("p t e -> p (t e)"),
                                 start=True, stop=False, skip_group_check=True)
                for t in range(NT - 1):
                    n = NT - 1 - t
                    mm = nc.tensor.matmul(m[:, (t + 1) * E:NT * E].rearrange("p (t e) -> p t e", e=E), onesb[:, :],
                                          onehot[:, t:t + 1, :].to_broadcast([P, n, E]), start=False,
                                          stop=(t == NT - 2), skip_group_check=True)
                mm.then_inc(full("route"), 1)

            def scores_by_query(k, i):
                b, g = divmod(k, NG)
                n = k * S1N + i
                if i == 0 and g == 0:
                    pe.wait_ge(parts_placed[b], 16 * placed_dmas(b))
                if n >= 2:
                    pe.wait_ge(s1_free, n - 1)
                pt = s1_bank[n % 2]
                blocks = query_blocks(g, i)
                w = (blocks[0][1] + 1) * P
                for j, (h, qt) in enumerate(blocks):
                    mm = nc.tensor.matmul(pt[:, j * w:(j + 1) * w], qs[:, b % 2, h, qt * P:(qt + 1) * P],
                                          ks[:, b % 2, h, 0:w], start=(j == 0), stop=(i < FUSED), skip_group_check=True)
                if i < FUSED:
                    mm.then_inc(s1_full, 1)
                    return
                c = len(blocks)
                diag = pt[:, 0:c * w].rearrange("p (c w) -> p c w", c=c)[:, :, w - P:w]
                neg = maskneg.rearrange("p (o k) -> p o k", o=1).to_broadcast([P, c, P])
                nc.tensor.matmul(diag, identb[:, :], neg, start=False, stop=True, skip_group_check=True)\
                    .then_inc(s1_full, 1)

            def scores_by_key(k, i):
                b, g = divmod(k, NG)
                n = k * S2N + i
                if i == 0:
                    pe.wait_ge(max_placed[k % 2], 16 * (k // 2 + 1))
                if n >= 3:
                    pe.wait_ge(s2_free, n - 2)
                pt = s2_bank[n % 3]
                h0 = g * G
                if i < G:
                    blocks = [(h0 + i, 0, 0)]
                elif i < 2 * G:
                    blocks = [(h0 + i - G, 1, 0), (h0 + i - G, 3, 3 * P)]
                else:
                    blocks = [(h0 + 2 * (i - 2 * G), 2, 0), (h0 + 2 * (i - 2 * G) + 1, 2, 2 * P)]
                for h, kb, at in blocks:
                    w = S - kb * P
                    mm = nc.tensor.matmul(pt[:, at:at + w], ks[:, b % 2, h, kb * P:(kb + 1) * P],
                                          qs[:, b % 2, h, kb * P:S], start=True, stop=True, skip_group_check=True)
                mm.then_inc(s2_full, 1)

            def probs_of(par, j, kb):
                if kb == 0:
                    return probs[:, par, j, :]
                if kb == 1:
                    return probs[:, par, G + j, 0:3 * P]
                if kb == 3:
                    return probs[:, par, G + j, 3 * P:4 * P]
                return probs[:, par, 2 * G + j // 2, (j % 2) * 2 * P:(j % 2 + 1) * 2 * P]

            def weigh_values(k, kb):
                b, g = divmod(k, NG)
                final = QT - 2 if k == K - 1 else QT - 1
                pe.wait_ge(s2_free, k * S2N + (G, 2 * G, S2N, 2 * G)[kb])
                pe.wait_ge(masked, 4 * k + (1, 2, 4, 3)[kb])
                if kb == 0:
                    if k == 0:
                        pe.wait_ge(o_filled, 1)
                    else:
                        pe.wait_ge(o_copied, k)
                for j in range(G):
                    mm = nc.tensor.matmul(o_bank[32 * j:32 * j + HD + 1, kb * P:S], v_aug[:, b * QT + kb, g * G + j, :],
                                          probs_of(k % 2, j, kb), start=(kb == 0), stop=(kb == final),
                                          skip_group_check=True)
                if kb == final:
                    mm.then_inc(weighed, 1)

            def turn_o(k):
                m = take(f"oT{k}")
                pe.wait_ge(o_copied, k + 1)
                for t in range(QT):
                    mm = nc.tensor.transpose(m[:, t * P:(t + 1) * P], oT_sb[:, k % 2, t * P:(t + 1) * P], identf[:, :])
                mm.then_inc(full(f"oT{k}"), 1)

            def sum_values(b):
                m = take(f"cum{b}")
                pe.wait_ge(vpre_ready, 2 * b + 2)
                va = v_aug[:, b * QT:(b + 1) * QT, :, 0:HD].rearrange("p t h d -> p (t h) d")
                nc.tensor.matmul(m[:, :], upto[:, :], va, start=True, stop=False, skip_group_check=True)
                nc.tensor.matmul(m[:, P:2 * P], onesf[:, :], va[:, 0:H, :], start=False, stop=False,
                                 skip_group_check=True)
                nc.tensor.matmul(m[:, 2 * P:4 * P], onesf[:, :], v_pre[:, :, :].rearrange("p t d -> p (t d)"),
                                 start=False, stop=True, skip_group_check=True).then_inc(full(f"cum{b}"), 1)

            def turn_max(k):
                m = take(f"maxT{k}")
                pe.wait_ge(s1_free, (k + 1) * S1N)
                nc.tensor.transpose(m[0:G * QT, 0:P], mx[:, k % 2].rearrange("p h t -> p (h t)"), identf[:, :])\
                    .then_inc(full(f"maxT{k}"), 1)

            def turn_blocks(name, source, at):
                m = take(name)
                for j in range(4):
                    mm = nc.tensor.transpose(m[:, j * P:(j + 1) * P], source(at + j), identf[:, :])
                mm.then_inc(full(name), 1)

            def expert_hidden(e, c):
                if c == 0:
                    pe.wait_ge(w_ring[e % WR], 32 * (e // WR + 1))
                    if e == 0:
                        for i in range(SB // 4):
                            wait_free(pe, f"slotT{i}")
                m = take(f"hid{e}_{c}")
                for j in range(2):
                    at = (2 * c + j) * P
                    mm = nc.tensor.matmul(m[:, j * CAP:(j + 1) * CAP], w1_sb[:, e % WR, at:at + P],
                                          slot_xT[:, e * CAP:(e + 1) * CAP], start=True, stop=True,
                                          skip_group_check=True)
                mm.then_inc(full(f"hid{e}_{c}"), 1)

            def expert_result(e):
                m = take(f"res{e}")
                for c in range(2):
                    wait_free(pe, f"hid{e}_{c}")
                for c in range(FC):
                    mm = nc.tensor.matmul(m[:, 0:CAP], w2_sb[:, e % WR, c, :], hid[:, e % 2, c, :],
                                          start=(c == 0), stop=(c == FC - 1))
                mm.then_inc(full(f"res{e}"), 1)

            def turn_attn(b):
                m = take(f"attT{b}")
                pe.wait_ge(attn_ready, (b + 1) * NG)
                for t in range(QT):
                    mm = nc.tensor.transpose(m[:, t * P:(t + 1) * P], attn[:, b * QT + t, :], identf[:, :])
                mm.then_inc(full(f"attT{b}"), 1)

            def project_attn(b):
                m = take(f"proj{b}")
                wait_free(pe, f"attT{b}")
                if b == 0:
                    pe.wait_ge(wc_loaded, 16)
                for t in range(QT):
                    mm = nc.tensor.matmul(m[:, t * P:(t + 1) * P], att_T[:, t * P:(t + 1) * P], wc[:, :],
                                          start=True, stop=True, skip_group_check=True)
                mm.then_inc(full(f"proj{b}"), 1)

            def part(k, kind, arg):
                if kind == "s2":
                    scores_by_key(k, arg)
                elif kind == "s1":
                    scores_by_query(k + LAG, arg)
                elif kind == "v":
                    project_v(arg)
                elif kind == "route_b":
                    count_ahead()
                elif kind == "weigh":
                    weigh_values(*arg)
                elif kind == "qk":
                    project_qk(*arg)
                elif kind == "slotT":
                    pe.wait_ge(slots_loaded, 16)
                    turn_blocks(f"slotT{arg}", lambda s: slot_sb[:, s, :], 4 * arg)
                elif kind == "hid":
                    expert_hidden(*arg)
                elif kind == "res":
                    expert_result(arg)
                elif kind == "resT":
                    if arg == 0:
                        for e in (E - 2, E - 1):
                            wait_free(pe, f"res{e}")
                    turn_blocks(f"resT{arg}", lambda s: slot_xT[:, s * P:(s + 1) * P], 4 * arg)
                elif kind == "oT":
                    turn_o(arg)
                elif kind == "cum":
                    sum_values(arg)
                elif kind == "maxT":
                    turn_max(arg)
                elif kind == "attT":
                    turn_attn(arg)
                elif kind == "proj":
                    project_attn(arg)

            for k in STAGES:
                for kind, arg in orders[k]:
                    part(k, kind, arg)
            turn_o(K - 1)
            turn_attn(B - 1)
            project_attn(B - 1)

        @block.vector
        def _(dve):
            ln = [0]

            def ln_count(ins):
                ln[0] += 1
                ins.then_inc(ln_step, 1)
                return ln[0]

            def deviations(batches):
                tiles = range(batches[0] * QT, (batches[-1] + 1) * QT)
                ts = slice(tiles[0], tiles[-1] + 1)
                for t in tiles:
                    if t % QT == 0:
                        dve.wait_ge(x_loaded[t // QT], 16)
                    n = ln_count(nc.vector.bn_stats(stats[:, t, :], x_sb[:, t, :]))
                first = n - len(tiles) + 1
                for j, t in enumerate(tiles):
                    dve.wait_ge(ln_step, first + j)
                    n = ln_count(nc.vector.bn_aggr(mv[:, t, :], stats[:, t, :]))
                dve.wait_ge(ln_step, n)
                turn = 0 if batches[0] == 0 else 1
                nc.vector.tensor_scalar(rstd[:, 0, ts], mv[:, ts, 1], 1e-5, None, ALU.add).then_inc(var_ready, 1)
                dve.wait_ge(std_ready, turn + 1)
                n = ln_count(nc.vector.reciprocal(rstd[:, 2, ts], rstd[:, 1, ts]))
                dve.wait_ge(ln_step, n)
                n = ln_count(nc.vector.tensor_tensor(rstd[:, 1, ts], rstd[:, 2, ts], rstd[:, 2, ts], ALU.mult))
                dve.wait_ge(ln_step, n)
                n = ln_count(nc.vector.tensor_tensor(rstd[:, 3, ts], rstd[:, 1, ts], rstd[:, 0, ts], ALU.mult))
                dve.wait_ge(ln_step, n)
                n = ln_count(nc.vector.tensor_scalar(rstd[:, 1, ts], rstd[:, 3, ts], -0.5, 1.5, ALU.mult, ALU.add))
                dve.wait_ge(ln_step, n)
                nc.vector.tensor_tensor(rstd[:, 0, ts], rstd[:, 2, ts], rstd[:, 1, ts], ALU.mult).then_inc(rstd_ready, 1)

            def split_rest(b, i):
                m = wait_full(dve, f"{'qk'[i]}{b}")
                dve.wait_ge(hi_ready, 2 * b + i + 1)
                nc.vector.scalar_tensor_tensor(out=rest[:, i, :], in0=m[:, :], scalar=bias[:, i:i + 1],
                                               in1=parts[:, i, 0, :], op0=ALU.add, op1=ALU.subtract)\
                    .then_inc(free(f"{'qk'[i]}{b}"), 1)

            def normalise_x(b):
                dve.wait_ge(rstd_ready, 2 if b else 1)
                for t in range(b * QT, (b + 1) * QT):
                    ins = nc.vector.tensor_scalar(xn[:, t, :], x_sb[:, t, :], mv[:, t, 0:1], rstd[:, 0, t:t + 1],
                                                  ALU.subtract, ALU.mult)
                ins.then_inc(xn_ready[b], 1)

            deviations(range(1))
            normalise_x(0)
            deviations(range(1, B))
            for i in range(2):
                split_rest(0, i)
            normalise_x(1)
            split_lo(dve, nc.vector, 0)
            for b in range(2, B):
                normalise_x(b)
            nc.vector.memset(o_bank[:, :], 0.0).then_inc(o_filled, 1)

            steps = [0]

            def step(ins):
                steps[0] += 1
                ins.then_inc(route_step, 1)
                dve.wait_ge(route_step, steps[0])

            def by_token(v):
                return v.rearrange("p (t o) -> p t o", o=1).to_broadcast([P, NT, E])

            def by_expert(v):
                return v.rearrange("p (o e) -> p o e", o=1).to_broadcast([P, NT, E])

            def choose_experts():
                dve.wait_ge(consts_ready, 2)
                for i in (VB - 2, VB - 1):
                    wait_free(dve, f"v{i}")
                step(nc.vector.tensor_reduce(rtc[:, 0, :], lg[:, :, :], AX.X, ALU.max))
                nc.vector.tensor_tensor(rt[:, 0], lg[:, :, :], by_token(rtc[:, 0, :]), ALU.subtract)\
                    .then_inc(gate_shift_ready, 1)
                step(nc.vector.tensor_tensor(rt[:, 2], lg[:, :, :], by_token(rtc[:, 0, :]), ALU.is_equal))
                step(nc.vector.scalar_tensor_tensor(out=lg[:, :, :], in0=rt[:, 2], scalar=-float(E), in1=by_expert(ev[:, :]),
                                                    op0=ALU.mult, op1=ALU.add))
                step(nc.vector.tensor_reduce(rtc[:, 1, :], lg[:, :, :], AX.X, ALU.min))
                step(nc.vector.tensor_scalar(rtc[:, 3, :], rtc[:, 1, :], float(E), None, ALU.add))
                nc.vector.tensor_tensor(onehot[:, :, :], by_expert(ev[:, :]), by_token(rtc[:, 3, :]), ALU.is_equal)\
                    .then_inc(onehot_ready, 1)

            def number_slots():
                dve.wait_ge(gate_exp_ready, 1)
                step(nc.vector.tensor_reduce(rtc[:, 4, :], rt[:, 1], AX.X, ALU.add))
                nc.vector.reciprocal(rtc[:, 2, :], rtc[:, 4, :]).then_inc(prob_ready, 1)
                dve.wait_ge(onehot_ready, 1)
                m = wait_full(dve, "route")
                nc.vector.tensor_tensor(rt[:, 2], m[:, 0:NT * E].rearrange("p (t e) -> p t e", e=E), onehot[:, :, :],
                                        ALU.mult).then_inc(free("route"), 1)
                wait_free(dve, "route")
                step(nc.vector.tensor_reduce(rtc[:, 5, :], rt[:, 2], AX.X, ALU.add))
                step(nc.vector.tensor_scalar(rtc[:, 6, :], rtc[:, 5, :], float(CAP), DROPPED, ALU.is_ge, ALU.mult))
                step(nc.vector.scalar_tensor_tensor(out=rtc[:, 7, :], in0=rtc[:, 3, :], scalar=float(CAP),
                                                    in1=rtc[:, 5, :], op0=ALU.mult, op1=ALU.add))
                step(nc.vector.tensor_tensor(rtc[:, 5, :], rtc[:, 7, :], rtc[:, 6, :], ALU.add))
                nc.vector.tensor_scalar(idx[:, :], rtc[:, 5, :], float(E * CAP), None, ALU.add).then_inc(idx_ready, 1)
                dve.wait_ge(gains_loaded, 48)
                nc.vector.tensor_copy(inv_row[:, 0, :], row_i[:, :]).then_inc(cum_gain_step, 1)
                dve.wait_ge(cum_gain_step, 1)
                nc.vector.reciprocal(inv_row[:, 1, :], inv_row[:, 0, :]).then_inc(cum_gain_step, 1)
                dve.wait_ge(cum_gain_step, 2)
                nc.vector.tensor_tensor(cum_gain[:, :, :],
                                        inv_row[:, 1, :].rearrange("p (t o) -> p t o", o=1).to_broadcast([P, QT, H]),
                                        gains[:, 2, :].rearrange("p (o h) -> p o h", o=1).to_broadcast([P, QT, H]),
                                        ALU.mult).then_inc(cum_gain_step, 1)

            def row_maxima(k, i):
                n = k * S1N + i
                dve.wait_ge(s1_full, n + 1)
                blocks = query_blocks(0, i)
                w = (blocks[0][1] + 1) * P
                h0, qt = blocks[0]
                c = len(blocks)
                if i < FUSED:
                    for j, (h, qt) in enumerate(blocks):
                        bank = s1_bank[n % 2][:, j * w:(j + 1) * w]
                        ins = nc.vector.tensor_tensor_reduce(bank, bank, causal[:, S - w:S], 1.0, NEG, ALU.add, ALU.max,
                                                             mx[:, k % 2, h, qt:qt + 1])
                    ins.then_inc(s1_free, 1)
                    return
                nc.vector.tensor_reduce(mx[:, k % 2, h0:h0 + c, qt], s1_bank[n % 2][:, 0:c * w].rearrange("p (c w) -> p c w", c=c),
                                        AX.X, ALU.max).then_inc(s1_free, 1)

            def normalise(k):
                b, g = divmod(k, NG)
                m = wait_full(dve, f"oT{k}")
                ov = m[:, :].rearrange("p (t j r) -> p t j r", t=QT, j=G)
                nc.vector.reciprocal(rec[:, :, :], ov[:, :, :, HD]).then_inc(norm_step, 1)
                dve.wait_ge(norm_step, 2 * k + 1)
                gain = gains[:, 0, g * G:(g + 1) * G].rearrange("p (o j) -> p o j", o=1).to_broadcast([P, QT, G])
                nc.vector.tensor_tensor(recg[:, :, :], rec[:, :, :], gain, ALU.mult).then_inc(norm_step, 1)
                dve.wait_ge(norm_step, 2 * k + 2)
                weight = recg[:, :, :].rearrange("p t (j o) -> p t j o", o=1).to_broadcast([P, QT, G, HD])
                nc.vector.tensor_tensor(onorm[:, :, :, :], ov[:, :, :, 0:HD], weight, ALU.mult).then_inc(free(f"oT{k}"), 1)
                wait_free(dve, f"oT{k}")
                if g == 0:
                    dve.wait_ge(base_ready, b + 1)
                av = attn[:, b * QT:(b + 1) * QT, g * G * HD:(g + 1) * G * HD].rearrange("p t (j d) -> p t j d", j=G)
                nc.vector.tensor_tensor(av, av, onorm[:, :, :, :], ALU.add).then_inc(attn_ready, 1)

            def take_off_means(b):
                m = wait_full(dve, f"cum{b}")
                gain = cum_gain[:, :, :].rearrange("p t h -> p (t h)").rearrange("p (n o) -> p n o", o=1).to_broadcast([P, QT * H, HD])
                if b == 0:
                    dve.wait_ge(cum_gain_step, 3)
                nc.vector.tensor_tensor(cum_part[:, :, :, :].rearrange("p t h d -> p (t h) d"),
                                        m[:, :].rearrange("p (n d) -> p n d", d=HD), gain, ALU.mult)\
                    .then_inc(free(f"cum{b}"), 1)
                wait_free(dve, f"cum{b}")
                dve.wait_ge(skip_ready, b + 1)
                av = attn[:, b * QT:(b + 1) * QT, :].rearrange("p t d -> p (t d)")
                nc.vector.tensor_tensor(av, av, cum_part[:, :, :, :].rearrange("p t h d -> p (t h d)"), ALU.subtract)\
                    .then_inc(base_ready, 1)

            def finish(b):
                m = wait_full(dve, f"proj{b}")
                dve.wait_ge(silu_ready, b + 1)
                if b >= 2:
                    dve.wait_ge(y_stored[b % 2], 16 * (b // 2))
                fv = fg[:, b * QT:(b + 1) * QT, :].rearrange("p t d -> p (t d)")
                nc.vector.tensor_tensor(y_sb[:, b % 2, :], m[:, :], fv, ALU.mult).then_inc(free(f"proj{b}"), 1)
                wait_free(dve, f"proj{b}")
                xv = x_sb[:, b * QT:(b + 1) * QT, :].rearrange("p t d -> p (t d)")
                nc.vector.tensor_tensor(y_sb[:, b % 2, :], y_sb[:, b % 2, :], xv, ALU.add).then_inc(y_ready, 1)

            def part(k, kind, arg):
                if kind == "s1":
                    row_maxima(k + LAG, arg)
                elif kind == "route_a":
                    choose_experts()
                elif kind == "route_b":
                    number_slots()
                elif kind == "qk":
                    split_rest(*arg)
                elif kind == "res":
                    m = wait_full(dve, f"res{arg}")
                    nc.vector.tensor_copy(slot_xT[:, arg * CAP:(arg + 1) * CAP], m[:, 0:CAP]).then_inc(free(f"res{arg}"), 1)
                elif kind == "resT":
                    m = wait_full(dve, f"resT{arg}")
                    nc.vector.tensor_copy(slot_sb[:, 4 * arg:4 * arg + 4, :].rearrange("p k d -> p (k d)"), m[:, :])\
                        .then_inc(free(f"resT{arg}"), 1)
                elif kind == "oT":
                    normalise(arg)
                elif kind == "cum":
                    take_off_means(arg)
                elif kind == "maxT":
                    m = wait_full(dve, f"maxT{arg}")
                    dve.wait_ge(nm_hi_ready, arg + 1)
                    nc.vector.scalar_tensor_tensor(out=mrest[:, :], in0=m[0:G * QT, 0:P], scalar=-1.0,
                                                   in1=negm[:, arg % 2, 0, :], op0=ALU.mult, op1=ALU.subtract)\
                        .then_inc(free(f"maxT{arg}"), 1)
                elif kind == "max_low":
                    dve.wait_ge(nm_mid_ready, arg + 1)
                    nc.vector.tensor_tensor(negm[:, arg % 2, 2, :], mrest[:, :], negm[:, arg % 2, 1, :], ALU.subtract)\
                        .then_inc(nm_lo_ready, 1)
                elif kind == "proj":
                    finish(arg)
                elif kind == "copy_o" and k + LAG >= K:
                    copy_o(dve, arg)
                elif kind == "attT" and k + LAG >= K:
                    copy_attT(dve, arg)

            for k in STAGES:
                for kind, arg in orders[k]:
                    part(k, kind, arg)
            normalise(K - 1)
            copy_attT(dve, B - 1)
            finish(B - 1)


_INS = ["L0_attn_x", "L0_attn_qk_w", "L0_attn_qk_b", "L0_attn_v_w", "L0_attn_cproj_w", "L0_attn_resid_gain",
        "L0_attn_skip_gain", "L0_attn_centre_gain", "L0_ffn_gate_w", "L0_ffn_w1", "L0_ffn_w2"]


def kernel(**inputs):
    import numpy as _np
    import concourse.bacc as _bacc
    from concourse import mybir as _mybir
    from concourse.bass_utils import run_bass_kernel_spmd as _run

    nc = _bacc.Bacc("TRN2", target_bir_lowering=False, num_devices=1)
    arrays, args = {}, []
    for name in _INS:
        a = _np.ascontiguousarray(inputs[name])
        arrays[f"in_{name}"] = a
        args.append(nc.dram_tensor(f"in_{name}", a.shape, _mybir.dt.from_np(a.dtype), kind="ExternalInput").ap())
    shape = inputs["L0_attn_x"].shape
    args.append(nc.dram_tensor("out_0", shape, _mybir.dt.float32, kind="ExternalOutput").ap())
    attention_moe_block(nc, *args)
    r = _run(nc, [arrays], core_ids=[0])
    return r.results[0]["out_0"]
```

```python
from contextlib import ExitStack

import numpy as np

import concourse.bass as bass
from concourse import mybir

F32 = mybir.dt.float32
BF16 = mybir.dt.bfloat16
I32 = mybir.dt.int32
U32 = mybir.dt.uint32
ALU = mybir.AluOpType
ACT = mybir.ActivationFunctionType
AX = mybir.AxisListType

P = 128
NEG = -1.0e30
ONE_ONE = float(np.array([0x3F803F80], np.uint32).view(np.float32)[0])
DROPPED = 1.0e6


def attention_moe_block(nc, x, qk_w, qk_b, v_w, cproj_w, resid_gain, skip_gain, centre_gain, gate_w, w1, w2, out):
    B, S, D = x.shape
    H = resid_gain.shape[1]
    HD = D // H
    E, _, F = w1.shape
    T = B * S
    CAP = int(1.25 * T / E)
    NT = T // P
    QT = S // P
    G = 4
    NG = H // G
    FC = F // P
    SLOTS = E * CAP
    SB = SLOTS // P
    PAIRS = 6
    R = PAIRS * HD
    MR = R + 3
    S1N = 2 * G + G // 2 + 1
    FUSED = 2 * G
    S2N = 2 * G + G // 2
    VB = (NT + 2) // 3
    WR = 3
    PART_PAIRS = ((0, 0), (0, 1), (1, 0), (1, 1), (0, 2), (2, 0))
    SCALE = float(HD) ** -0.5
    assert D == P and S == 4 * P and HD == 8 and H == 16 and SLOTS % P == 0

    K = B * NG
    LAG = 2
    STAGES = range(-LAG, K)
    WARM_FIRST, WARM_SECOND = 9, 1
    AHEAD, AHEAD_FROM = 1, 64
    V_AHEAD = 1
    V_AT = 2
    ROUTE_A, ROUTE_B = 7, 10
    COUNT_APART = 3
    FIND_AT = 1
    SCATTER_AT, SCATTER_EVERY = 5, 2
    QK1_AT = 7
    QK_AT = 4
    QK_APART, LOW_APART = 0, 0
    PLACE_APART, PLACE_WAIT = 2, -2
    MAX_AT, MAX_APART = 1, 1
    WEIGH_AT = (0, 4, 6, 6)
    COPY_AT, TURN_AT = 6, 8
    LAST_WEIGH_AT = (0, 2, 3, 3)
    LAST_COPY_AT, LAST_TURN_AT = 4, 6
    FINAL_AT = (10, 10, 10, 10)
    CUM_AT = 10
    SLOTS_AT = 1 * S1N + 9
    SLOTS_TURN = 2 * S1N + 4
    FFN_AT = 3 * S1N + 1
    FFN_EVERY = 3.5
    RES_APART = 3
    RES_TURN = 8 * S1N + 5
    CLEAR_AT = 2 * S1N + 6
    SILU_AT = 13
    SILU_STEP, PAUSE = 0, 5
    GATHER_AT, GATHER_EVERY = 102, 2
    GATE_AT, GATE_EVERY = 135, 2
    PREFIX0_AT = 4
    PREFIX_AT = 1 * S1N + 4
    FIRST_TURN, FIRST_PROJ = 7, 9
    ATT_TURN, ATT_PROJ = 4, 7
    S1_BANKS, S2_BANKS = 3, 2
    tasks = {}

    def place(kind, arg, step):
        tasks.setdefault(step, []).append((kind, arg))

    start = -LAG * S1N
    for i in range(V_AHEAD, VB):
        place("v", i, start + V_AT + i - V_AHEAD)
    place("prefix", 0, start + PREFIX0_AT)
    for j in range(6):
        place("choose", j, start + ROUTE_A)
    place("gate_exp", 0, start + ROUTE_A + 5)
    place("count", 0, start + ROUTE_A + COUNT_APART)
    for j in range(5):
        place("number", j, start + ROUTE_B)
    for j in range(3):
        place("find", j, FIND_AT + j)
    for t in range(NT):
        place("scatter", t, start + SCATTER_AT + t * SCATTER_EVERY)
    for b in range(1, B):
        at = QK1_AT if b == 1 else ((b - 1) * NG - 1) * S1N + QK_AT
        place("qk", (b, 0), at)
        place("qk", (b, 1), at + QK_APART)
        place("qk_low", b, at + QK_APART + LOW_APART)
        place("place", b, at + QK_APART + PLACE_APART if b == 1 else (b - 1) * NG * S1N + PLACE_WAIT)
        place("prefix", b, (b - 1) * NG * S1N + PREFIX_AT)
    for k in range(K):
        place("maxT", k, (k - 1) * S1N + MAX_AT)
        place("max_low", k, (k - 1) * S1N + MAX_AT + MAX_APART)
    for k in range(K - 1):
        last = k == K - 2
        at = (k + 1) * S1N
        for kb, step in enumerate(LAST_WEIGH_AT if last else WEIGH_AT):
            place("weigh", (k, kb), at + step)
        place("copy_o", k, at + (LAST_COPY_AT if last else COPY_AT))
        place("oT", k, at + (LAST_TURN_AT if last else TURN_AT))
    for kb, step in zip((0, 1, 3, 2), FINAL_AT):
        place("weigh", (K - 1, kb), (K - 1) * S1N + step)
    place("copy_o", K - 1, K * S1N - 1)
    for b in range(B):
        place("cum", b, b * NG * S1N + CUM_AT)
    place("slots_load", 0, SLOTS_AT)
    for i in range(SB // 4):
        place("slotT", i, SLOTS_TURN + i)
    for e in range(E):
        at = FFN_AT + int(e * FFN_EVERY)
        place("hid", (e, 0), at)
        place("hid", (e, 1), at + 1)
        place("res", e, at + RES_APART)
    for i in range(SB // 4):
        place("resT", i, RES_TURN + i)
    place("clear", 0, CLEAR_AT)
    for t in range(NT):
        place("gather", t, GATHER_AT + int(t * GATHER_EVERY))
    for b in range(B):
        place("gate", b, GATE_AT + b * GATE_EVERY)
    for b in range(1, B - 1):
        place("attT", b, (SILU_AT + b) * S1N + ATT_TURN)
        place("proj", b, (SILU_AT + b) * S1N + ATT_PROJ)
    place("attT", 0, SILU_AT * S1N + FIRST_TURN)
    place("proj", 0, SILU_AT * S1N + FIRST_PROJ)

    first_pass = {}
    for n in range(K * S1N):
        ahead = AHEAD if n >= AHEAD_FROM else 0
        first_pass.setdefault(n - LAG * S1N - ahead, []).append(("s1", divmod(n, S1N)))

    def stage_order(k):
        order, banks = [], list(range(S2N)) if k >= 0 else []
        for i in range(S1N):
            pause = k == SILU_AT and SILU_STEP < i <= SILU_STEP + PAUSE
            behind = len(banks) > S2N - i
            for _ in range(0 if pause else 2 if behind else 1):
                if banks:
                    order.append(("s2", banks.pop(0)))
            order += first_pass.get(k * S1N + i, ())
            order += tasks.get(k * S1N + i, ())
            if (k, i) == (SILU_AT, SILU_STEP):
                order.append(("silu", 0))
        return order + [("s2", i) for i in banks]

    orders = {k: stage_order(k) for k in STAGES}

    uses = ["xT0", "columns", "q0", "k0"] + [f"v{i}" for i in range(V_AHEAD)] + [f"xT{b}" for b in range(1, B)]
    for k in STAGES:
        for kind, arg in orders[k]:
            if kind == "qk":
                uses.append(f"{'qk'[arg[1]]}{arg[0]}")
            elif kind == "hid":
                uses.append(f"hid{arg[0]}_{arg[1]}")
            elif kind == "count":
                uses.append("route")
            elif kind in ("v", "maxT", "slotT", "res", "resT", "oT", "cum", "attT", "proj"):
                uses.append(f"{kind}{arg}")
    uses += [f"oT{K - 1}"] + [f"{kind}{B - 1}_{half}" for kind in ("attT", "proj") for half in range(2)]
    use_of = {name: n for n, name in enumerate(uses)}

    with ExitStack() as ctx:
        def sb(name, shape, dt=F32):
            return ctx.enter_context(nc.sbuf_tensor(name, shape, dt))

        def sem(name):
            return ctx.enter_context(nc.semaphore(name))

        def dram(name, shape, dt):
            return nc.dram_tensor(name, shape, dt, kind="Internal").ap()

        max_rows = dram("max_rows", [K, 3, G, S], BF16)
        slot_rows = dram("slot_rows", [SLOTS, D], F32)
        result_rows = dram("result_rows", [SLOTS, D], F32)

        stack = sb("stack", [P, 2, H, 2, S], BF16)
        qs, ks = stack[:, :, :, 0, :], stack[:, :, :, 1, :]
        probs = sb("probs", [P, 2, S2N, S])
        x_sb = sb("x_sb", [P, NT, D])
        xn = sb("xn", [P, NT, D])
        fg = xn
        slot_xT = sb("slot_xT", [P, SLOTS])
        slot_sb = sb("slot_sb", [P, SB, D])
        v_aug = sb("v_aug", [P, NT, H, HD + 1])
        v_pre = sb("v_pre", [P, 2, D])
        w1_sb = sb("w1_sb", [P, WR, F])
        w2_sb = sb("w2_sb", [P, WR, FC, D])
        hid = sb("hid", [P, 2, FC, CAP])
        parts = sb("parts", [P, 2, 3, S], BF16)
        rest = sb("rest", [P, 2, S])
        attn = sb("attn", [P, NT, D])
        xnT = [slot_xT[:, b * S:(b + 1) * S] for b in range(2)]
        xnT += [attn[:, b * QT:(b + 1) * QT, :].rearrange("p t d -> p (t d)") for b in range(2, B)]
        warm = sb("warm", [P, 1])
        oT_sb = sb("oT_sb", [P, 2, S])
        att_T = sb("att_T", [P, S])
        y_sb = rest
        wqk = sb("wqk", [P, 2, HD, H])
        wqk_raw = att_T[:, 0:2 * D]
        brow_raw = att_T[0:1, 2 * D:4 * D]
        wvg = sb("wvg", [P, D + E])
        wc = sb("wc", [P, D])
        gate_sb = sb("gate_sb", [E, D])
        brow = sb("brow", [1, 2, HD, H])
        bias = sb("bias", [P, 2])
        gains = sb("gains", [P, 3, H])
        identf = sb("identf", [P, P])
        identb = sb("identb", [P, P], BF16)
        causal = sb("causal", [P, S], BF16)
        maskneg = causal[:, S - P:S]
        before = sb("before", [P, P], BF16)
        onesb = sb("onesb", [P, P], BF16)
        upto = sb("upto", [P, P])
        onesf = sb("onesf", [P, P])
        stats = sb("stats", [P, NT, 6])
        mv = sb("mv", [P, NT, 2])
        rstd = sb("rstd", [P, 4, NT])
        lg = sb("lg", [P, NT, E])
        rt = oT_sb[:, :, :].rearrange("p a t -> p (a t)")[:, 0:3 * NT * E].rearrange("p (a t e) -> p a t e", a=3, t=NT)
        rtc = sb("rtc", [P, 8, NT])
        onehot = sb("onehot", [P, NT, E], BF16)
        ev = sb("ev", [P, E])
        idx = sb("idx", [P, NT], I32)
        row_i = sb("row_i", [P, QT], I32)
        inv_row = sb("inv_row", [P, 2, QT])
        mx = sb("mx", [P, 2, G, QT])
        negm = sb("negm", [G * QT, 2, 3, P], BF16)
        mrest = sb("mrest", [G * QT, P])
        rec = sb("rec", [P, QT, G])
        recg = sb("recg", [P, QT, G])
        onorm = sb("onorm", [P, QT, G, HD])
        cum_gain = sb("cum_gain", [P, QT, H])
        cum_part = sb("cum_part", [P, QT, H, HD])

        def bank(name):
            return ctx.enter_context(nc.psum_tensor(name, [P, 512], F32))

        s1_bank = [bank(f"s1_bank{i}") for i in range(S1_BANKS)]
        s2_bank = [bank(f"s2_bank{i}") for i in range(S2_BANKS)]
        o_bank = bank("o_bank")
        mi_bank = [bank(f"mi_bank{i}") for i in range(2)]

        x_loaded = [sem(f"x_loaded{b}") for b in range(B)]
        small_loaded = sem("small_loaded")
        wqk_loaded = sem("wqk_loaded")
        wv_loaded = sem("wv_loaded")
        brow_turned = sem("brow_turned")
        wqk_turned = sem("wqk_turned")
        wc_loaded = sem("wc_loaded")
        gains_loaded = sem("gains_loaded")
        const_step = sem("const_step")
        consts_ready = sem("consts_ready")
        q_filled = [sem(f"q_filled{i}") for i in range(2)]
        k_filled = sem("k_filled")
        slots_filled = sem("slots_filled")
        o_filled = sem("o_filled")
        ones_filled = sem("ones_filled")
        ln_step = sem("ln_step")
        var_ready = sem("var_ready")
        std_ready = sem("std_ready")
        rstd_ready = sem("rstd_ready")
        xn_ready = [sem(f"xn_ready{b}") for b in range(B)]
        mi_full = [sem(f"mi_full{i}") for i in range(2)]
        mi_free = [sem(f"mi_free{i}") for i in range(2)]
        wvg_ready = sem("wvg_ready")
        hi_ready = sem("hi_ready")
        mid_ready = sem("mid_ready")
        lo_ready = sem("lo_ready")
        parts_placed = [sem(f"parts_placed{b}") for b in range(B)]
        v_ready = sem("v_ready")
        vpre_ready = sem("vpre_ready")
        route_step = sem("route_step")
        onehot_ready = sem("onehot_ready")
        gate_shift_ready = sem("gate_shift_ready")
        gate_exp_ready = sem("gate_exp_ready")
        prob_ready = sem("prob_ready")
        idx_ready = sem("idx_ready")
        slots_cleared = sem("slots_cleared")
        scattered = sem("scattered")
        slots_loaded = sem("slots_loaded")
        w_ring = [sem(f"w_ring{i}") for i in range(WR)]
        results_stored = sem("results_stored")
        fg_cleared = sem("fg_cleared")
        gathered = [sem(f"gathered{b}") for b in range(B)]
        silu_ready = sem("silu_ready")
        s1_full = sem("s1_full")
        s1_free = sem("s1_free")
        s2_full = sem("s2_full")
        s2_free = sem("s2_free")
        masked = sem("masked")
        weighed = sem("weighed")
        o_copied = sem("o_copied")
        nm_hi_ready = sem("nm_hi_ready")
        nm_mid_ready = sem("nm_mid_ready")
        nm_lo_ready = sem("nm_lo_ready")
        max_stored = [sem(f"max_stored{i}") for i in range(2)]
        max_placed = [sem(f"max_placed{i}") for i in range(2)]
        cum_gain_step = sem("cum_gain_step")
        skip_ready = sem("skip_ready")
        base_ready = sem("base_ready")
        norm_step = sem("norm_step")
        attn_ready = sem("attn_ready")
        gated = sem("gated")
        y_ready = sem("y_ready")
        y_stored = [sem(f"y_stored{i}") for i in range(2)]

        def take(name):
            n = use_of[name]
            if n >= 2:
                nc.tensor.wait_ge(mi_free[n % 2], n // 2)
            return mi_bank[n % 2]

        def full(name):
            return mi_full[use_of[name] % 2]

        def free(name):
            return mi_free[use_of[name] % 2]

        def wait_full(eng, name):
            eng.wait_ge(full(name), use_of[name] // 2 + 1)
            return mi_bank[use_of[name] % 2]

        def wait_free(eng, name):
            eng.wait_ge(free(name), use_of[name] // 2 + 1)

        def wait_x_turned(eng, b):
            wait_free(eng, f"xT{b}")

        def share(kind, b, half):
            if half is None:
                return f"{kind}{b}", slice(0, QT)
            return f"{kind}{b}_{half}", slice(half * QT // 2, (half + 1) * QT // 2)

        def placed_dmas(b):
            return PAIRS + (1 if b >= 2 else 0)

        def query_blocks(g, i):
            if i < 2 * G:
                return [(g * G + i % G, QT - 1 - i // G)]
            if i < S1N - 1:
                return [(g * G + 2 * (i - 2 * G) + j, 1) for j in range(2)]
            return [(g * G + j, 0) for j in range(G)]

        def copy_out(eng, out, src):
            if eng is nc.vector:
                return nc.vector.tensor_copy(out, src)
            return nc.scalar.activation(out, src, ACT.Copy)

        def copy_o(eng, k):
            eng.wait_ge(weighed, k + 1)
            if k >= 2:
                wait_full(eng, f"oT{k - 2}")
            copy_out(eng, oT_sb[:, k % 2, :], o_bank[:, :]).then_inc(o_copied, 1)

        def copy_attT(eng, b, half=None):
            name, ts = share("attT", b, half)
            m = wait_full(eng, name)
            cols = slice(ts.start * P, ts.stop * P)
            copy_out(eng, att_T[:, cols], m[:, cols]).then_inc(free(name), 1)

        def split_lo(eng, engine, b):
            for i in range(2):
                eng.wait_ge(mid_ready, 2 * b + i + 1)
                engine.tensor_tensor(parts[:, i, 2, :], rest[:, i, :], parts[:, i, 1, :], ALU.subtract)\
                    .then_inc(lo_ready, 1)

        block = ctx.enter_context(nc.Block())

        @block.sync
        def _(sp):
            for b in range(B):
                sp.dma_start(x_sb[:, b * QT:(b + 1) * QT, :], x[b].rearrange("(t p) d -> p t d", p=P))\
                    .then_inc(x_loaded[b], 16)
                if b == 0:
                    sp.dma_start(wqk_raw, qk_w).then_inc(wqk_loaded, 16)
            sp.dma_start(wvg[:, 0:D], v_w).then_inc(wv_loaded, 16)
            sp.dma_start(wc[:, :], cproj_w).then_inc(wc_loaded, 16)
            for i, gain in enumerate((resid_gain, skip_gain, centre_gain)):
                sp.dma_start(gains[:, i, :], gain.rearrange("a h b c -> (a b c) h").to_broadcast([P, H]))\
                    .then_inc(gains_loaded, 16)

            by_part = parts[:, :, :, :].rearrange("p i c t -> p (i c) t")

            def place_parts(b):
                par = b % 2
                if b >= 2:
                    sp.wait_ge(s2_full, (b - 1) * NG * S2N)
                    sp.dma_start(qs[R:MR, par], qs[64:64 + MR - R, par]).then_inc(parts_placed[b], 16)
                else:
                    sp.wait_ge(q_filled[b], 1)
                    sp.wait_ge(k_filled, b + 1)
                for row, (cq, ck) in enumerate(PART_PAIRS):
                    if row == 0:
                        sp.wait_ge(hi_ready, 2 * b + 2)
                    elif row == 1:
                        sp.wait_ge(mid_ready, 2 * b + 2)
                    elif row == 4:
                        sp.wait_ge(lo_ready, 2 * b + 2)
                    rows = slice(row * HD, (row + 1) * HD)
                    sp.dma_start(stack[rows, par], by_part[:, cq:4 + ck:3 + ck - cq, :]).then_inc(parts_placed[b], 16)

            def load_expert(e):
                if e >= WR:
                    wait_full(sp, f"res{e - WR}")
                sp.dma_start(w1_sb[:, e % WR, :], w1[e]).then_inc(w_ring[e % WR], 16)
                sp.dma_start(w2_sb[:, e % WR], w2[e].rearrange("(c p) d -> p c d", p=P)).then_inc(w_ring[e % WR], 16)

            def place_max(k):
                sp.wait_ge(nm_lo_ready, k + 1)
                b, g = divmod(k, NG)
                sp.dma_start(max_rows[k].rearrange("c h (t q) -> (h t) c q", q=P), negm[:, k % 2])\
                    .then_inc(max_stored[k % 2], 16)
                sp.wait_ge(max_stored[k % 2], 16 * (k // 2 + 1))
                sp.dma_start(stack[R:MR, b % 2, g * G:(g + 1) * G, 0, :], max_rows[k]).then_inc(max_placed[k % 2], 16)

            def store_y(b, half=None):
                sp.wait_ge(y_ready, b + (half or 0) + 1)
                ts = share("proj", b, half)[1]
                sp.dma_start(out[b].rearrange("(t p) d -> p t d", p=P)[:, ts],
                             y_sb[:, b % 2, :].rearrange("p (t d) -> p t d", t=QT)[:, ts]).then_inc(y_stored[b % 2], 16)

            place_parts(0)
            sp.wait_ge(slots_filled, 1)
            sp.dma_start(slot_rows.rearrange("(k p) d -> p k d", p=P), slot_sb[:, :, :]).then_inc(slots_cleared, 16)
            for e in range(WR):
                load_expert(e)
            for k in STAGES:
                for kind, arg in orders[k]:
                    if kind == "max_low":
                        place_max(arg)
                    elif kind == "place":
                        place_parts(arg)
                    elif kind == "slots_load":
                        sp.wait_ge(scattered, 16 * NT)
                        sp.dma_start(slot_sb[:, :, :], slot_rows.rearrange("(k p) d -> p k d", p=P))\
                            .then_inc(slots_loaded, 16)
                    elif kind == "res" and arg + WR < E:
                        load_expert(arg + WR)
                    elif kind == "resT" and arg == SB // 4 - 1:
                        for i in range(SB // 4):
                            wait_free(sp, f"resT{i}")
                        sp.dma_start(result_rows.rearrange("(k p) d -> p k d", p=P), slot_sb[:, :, :])\
                            .then_inc(results_stored, 16)
                    elif kind == "proj":
                        store_y(arg)
            for half in range(2):
                store_y(B - 1, half)
            for i in range(2):
                sp.wait_ge(y_stored[i], 16 * (B // 2 + (i == (B - 1) % 2)))

        @block.gpsimd
        def _(pool):
            nc.gpsimd.memset(identf[:, :], 0.0).then_inc(const_step, 1)
            nc.gpsimd.memset(onesf[:, :], 1.0).then_inc(const_step, 1)
            nc.gpsimd.memset(onesb[:, :], 1.0).then_inc(const_step, 1)
            nc.gpsimd.memset(causal[:, :], 0.0).then_inc(const_step, 1)
            pool.wait_ge(const_step, 4)
            nc.gpsimd.affine_select(out=identf[:, :], in_=identf[:, :], compare_op=ALU.not_equal, fill=1.0,
                                    base=0, pattern=[[-1, P]], channel_multiplier=1).then_inc(const_step, 1)
            nc.gpsimd.affine_select(out=maskneg, in_=maskneg, compare_op=ALU.is_ge, fill=NEG,
                                    base=0, pattern=[[-1, P]], channel_multiplier=1)
            pool.wait_ge(const_step, 5)
            nc.gpsimd.tensor_copy(identb[:, :], identf[:, :]).then_inc(consts_ready, 1)
            nc.gpsimd.memset(ks[:, 0].bitcast(F32), ONE_ONE).then_inc(k_filled, 1)
            nc.gpsimd.memset(qs[:, 0].bitcast(F32), 0.0).then_inc(q_filled[0], 1)
            nc.gpsimd.affine_select(out=before[:, :], in_=onesb[:, :], compare_op=ALU.is_gt, fill=0.0,
                                    base=0, pattern=[[1, P]], channel_multiplier=-1)
            nc.gpsimd.affine_select(out=upto[:, :], in_=onesf[:, :], compare_op=ALU.is_ge, fill=0.0,
                                    base=0, pattern=[[1, P]], channel_multiplier=-1)
            nc.gpsimd.iota(ev[:, :], [[1, E]], base=-E, channel_multiplier=0,
                           allow_small_or_imprecise_dtypes=True)
            nc.gpsimd.iota(row_i[:, :], [[P, QT]], base=1, channel_multiplier=1).then_inc(consts_ready, 1)
            nc.gpsimd.memset(v_aug[:, :, :, HD:HD + 1], 1.0).then_inc(ones_filled, 1)
            nc.gpsimd.memset(slot_sb[:, :, :], 0.0).then_inc(slots_filled, 1)
            nc.gpsimd.memset(qs[:, 1].bitcast(F32), 0.0).then_inc(q_filled[1], 1)
            nc.gpsimd.memset(ks[:, 1].bitcast(F32), ONE_ONE).then_inc(k_filled, 1)

            def scatter(t):
                if t == 0:
                    pool.wait_ge(idx_ready, 1)
                    pool.wait_ge(slots_cleared, 16)
                pool.indirect_dma_start(
                    slot_rows, bass.IndirectOffsetOnAxis(ap=idx[:, t:t + 1].bitcast(U32), axis=0),
                    xn[:, t, :], None, bounds_check=SLOTS - 1, oob_is_err=False).then_inc(scattered, 16)

            def gather(t):
                if t == 0:
                    pool.wait_ge(fg_cleared, 1)
                    pool.wait_ge(results_stored, 16)
                pool.indirect_dma_start(
                    fg[:, t, :], None, result_rows,
                    bass.IndirectOffsetOnAxis(ap=idx[:, t:t + 1].bitcast(U32), axis=0),
                    bounds_check=SLOTS - 1, oob_is_err=False).then_inc(gathered[t // QT], 16)

            def prefix_values(b):
                if b == 0:
                    pool.wait_ge(v_ready, VB)
                    pool.wait_ge(gains_loaded, 48)
                else:
                    wait_full(pool, f"cum{b - 1}")
                    if b >= 2:
                        wait_full(pool, f"k{b}")
                va = v_aug[:, b * QT:(b + 1) * QT, :, 0:HD]
                pre = v_pre[:, :, :].rearrange("p t (h d) -> p t h d", h=H)
                nc.gpsimd.tensor_tensor(pre[:, 0], va[:, 0], va[:, 1], ALU.add).then_inc(vpre_ready, 1)
                pool.wait_ge(vpre_ready, 2 * b + 1)
                nc.gpsimd.tensor_tensor(pre[:, 1], pre[:, 0], va[:, 2], ALU.add).then_inc(vpre_ready, 1)
                for t in range(QT):
                    ins = nc.gpsimd.tensor_tensor(
                        attn[:, b * QT + t, :].rearrange("p (h d) -> p h d", h=H), va[:, t],
                        gains[:, 1, :].rearrange("p (h o) -> p h o", o=1).to_broadcast([P, H, HD]), ALU.mult)
                ins.then_inc(skip_ready, 1)

            def mask_probs(k, bank):
                blocks = probs[:, k % 2, :, :].rearrange("p u (c q) -> p (u c) q", q=P)
                for n, first, apart in ((G, 0, QT), (2 * G, G * QT, QT), (2 * G, G * QT + 3, QT), (S2N, 2 * G * QT, 2)):
                    if n == bank + 1:
                        pool.wait_ge(s2_free, k * S2N + n)
                        v = blocks[:, first:first + apart * (G - 1) + 1:apart, :]
                        nc.gpsimd.affine_select(out=v, in_=v, compare_op=ALU.is_ge, fill=0.0, base=0,
                                                pattern=[[0, G], [1, P]], channel_multiplier=-1).then_inc(masked, 1)

            def gate(b):
                pool.wait_ge(gathered[b], 16 * QT)
                if b == 0:
                    pool.wait_ge(prob_ready, 1)
                v = fg[:, b * QT:(b + 1) * QT, :]
                weight = rtc[:, 2, b * QT:(b + 1) * QT].rearrange("p (t o) -> p t o", o=1).to_broadcast([P, QT, D])
                nc.gpsimd.tensor_tensor(v, v, weight, ALU.mult).then_inc(gated, 1)

            for k in STAGES:
                for kind, arg in orders[k]:
                    if kind == "s2":
                        mask_probs(k, arg)
                    elif kind == "qk_low":
                        split_lo(pool, nc.gpsimd, arg)
                    elif kind == "prefix":
                        prefix_values(arg)
                    elif kind == "scatter":
                        scatter(arg)
                    elif kind == "clear":
                        pool.wait_ge(scattered, 16 * NT)
                        nc.gpsimd.memset(fg[:, :, :], 0.0).then_inc(fg_cleared, 1)
                    elif kind == "gather":
                        gather(arg)
                    elif kind == "gate":
                        gate(arg)

        @block.scalar
        def _(act):
            act.dma_start(gate_sb[:, :], gate_w).then_inc(small_loaded, 16)
            act.dma_start(brow_raw, qk_b.rearrange("(o n) -> o n", o=1)).then_inc(small_loaded, 16)
            act.wait_ge(const_step, 4)
            nc.scalar.activation(warm[:, :], onesf[:, 0:1], ACT.Sqrt)

            def deviation(turn):
                act.wait_ge(var_ready, turn + 1)
                ts = slice(turn * QT, NT if turn else QT)
                nc.scalar.activation(rstd[:, 1, ts], rstd[:, 0, ts], ACT.Sqrt).then_inc(std_ready, 1)

            def copy_xT(b):
                m = wait_full(act, f"xT{b}")
                nc.scalar.activation(xnT[b], m[:, :], ACT.Copy).then_inc(free(f"xT{b}"), 1)

            def split_hi(b, i):
                if b and i == 0:
                    act.wait_ge(parts_placed[b - 1], 16 * placed_dmas(b - 1))
                elif b == 0:
                    wait_free(act, "columns")
                m = wait_full(act, f"{'qk'[i]}{b}")
                nc.scalar.activation(parts[:, i, 0, :], m[:, :], ACT.Identity,
                                     bias=bias[:, i:i + 1]).then_inc(hi_ready, 1)

            def split_mid(b):
                for i, n in enumerate("qk"):
                    wait_free(act, f"{n}{b}")
                    nc.scalar.activation(parts[:, i, 1, :], rest[:, i, :], ACT.Copy).then_inc(mid_ready, 1)

            deviation(0)
            act.wait_ge(small_loaded, 32)
            nc.scalar.activation(brow[:, :, :, :], brow_raw.rearrange("o (i h d) -> o i d h", i=2, h=H), ACT.Copy)\
                .then_inc(brow_turned, 1)
            act.wait_ge(wqk_loaded, 16)
            nc.scalar.activation(wqk[:, :, :, :], wqk_raw.rearrange("p (i h d) -> p i d h", i=2, h=H), ACT.Copy)\
                .then_inc(wqk_turned, 1)
            copy_xT(0)
            m = wait_full(act, "columns")
            nc.scalar.activation(wvg[:, D:D + E], m[:, 0:E], ACT.Copy).then_inc(wvg_ready, 1)
            nc.scalar.activation(bias[:, :], m[:, E:E + 2], ACT.Copy).then_inc(free("columns"), 1)
            for i in range(2):
                split_hi(0, i)
            deviation(1)
            split_mid(0)

            def copy_values(i):
                m = wait_full(act, f"v{i}")
                n = min(3, NT - 3 * i)
                vg = m[:, 0:n * (D + E)].rearrange("p (t c) -> p t c", t=n)
                nc.scalar.activation(v_aug[:, 3 * i:3 * i + n, :, 0:HD],
                                     vg[:, :, 0:D].rearrange("p t (h d) -> p t h d", h=H), ACT.Copy).then_inc(v_ready, 1)
                nc.scalar.activation(lg[:, 3 * i:3 * i + n, :], vg[:, :, D:D + E], ACT.Copy).then_inc(free(f"v{i}"), 1)

            act.wait_ge(ones_filled, 1)
            for i in range(V_AHEAD):
                copy_values(i)
            for b in range(1, B):
                copy_xT(b)

            def exponential(k, i):
                n = k * S2N + i
                if i == 0 and k >= 2:
                    act.wait_ge(weighed, k - 1)
                act.wait_ge(s2_full, n + 1)
                nc.scalar.activation(probs[:, k % 2, i, :], s2_bank[n % S2_BANKS][:, :], ACT.Exp,
                                     scale=SCALE).then_inc(s2_free, 1)

            def part(k, kind, arg):
                if kind == "s2":
                    exponential(k, arg)
                elif kind == "v":
                    copy_values(arg)
                elif kind == "gate_exp":
                    act.wait_ge(gate_shift_ready, 1)
                    nc.scalar.activation(rt[:, 1], rt[:, 0], ACT.Exp).then_inc(gate_exp_ready, 1)
                elif kind == "qk":
                    split_hi(*arg)
                elif kind == "qk_low":
                    split_mid(arg)
                elif kind == "slotT":
                    m = wait_full(act, f"slotT{arg}")
                    nc.scalar.activation(slot_xT[:, arg * 4 * P:(arg + 1) * 4 * P], m[:, :], ACT.Copy)\
                        .then_inc(free(f"slotT{arg}"), 1)
                elif kind == "hid":
                    e, c = arg
                    m = wait_full(act, f"hid{e}_{c}")
                    nc.scalar.activation(hid[:, e % 2, 2 * c:2 * c + 2, :],
                                         m[:, 0:2 * CAP].rearrange("p (c s) -> p c s", c=2), ACT.Relu)\
                        .then_inc(free(f"hid{e}_{c}"), 1)
                elif kind == "copy_o" and k + LAG < K:
                    copy_o(act, arg)
                elif kind == "maxT":
                    m = wait_full(act, f"maxT{arg}")
                    if arg >= 2:
                        act.wait_ge(max_stored[arg % 2], 16 * (arg // 2))
                    nc.scalar.activation(negm[:, arg % 2, 0, :], m[0:G * QT, 0:P], ACT.Copy, scale=-1.0)\
                        .then_inc(nm_hi_ready, 1)
                elif kind == "max_low":
                    wait_free(act, f"maxT{arg}")
                    nc.scalar.activation(negm[:, arg % 2, 1, :], mrest[:, :], ACT.Copy).then_inc(nm_mid_ready, 1)
                elif kind == "silu":
                    for b in range(B):
                        act.wait_ge(gated, b + 1)
                        nc.scalar.activation(fg[:, b * QT:(b + 1) * QT, :], fg[:, b * QT:(b + 1) * QT, :], ACT.Silu)\
                            .then_inc(silu_ready, 1)
                elif kind == "attT" and k + LAG < K:
                    copy_attT(act, arg)

            for k in STAGES:
                for kind, arg in orders[k]:
                    part(k, kind, arg)
            copy_attT(act, B - 1, 0)

        @block.tensor
        def _(pe):
            def keep_clock(n):
                for _ in range(n):
                    nc.tensor.matmul(s1_bank[0][:, :], identb[:, :], causal[:, :], start=True, stop=True)

            def turn_x(b):
                pe.wait_ge(xn_ready[b], 1)
                m = take(f"xT{b}")
                for t in range(QT):
                    mm = nc.tensor.transpose(m[:, t * P:(t + 1) * P], xn[:, b * QT + t, :], identf[:, :])
                mm.then_inc(full(f"xT{b}"), 1)

            def project_qk(b, i):
                m = take(f"{'qk'[i]}{b}")
                wait_x_turned(pe, b)
                w = wqk[:, i].rearrange("p d h -> p (d h)")
                nc.tensor.matmul(m[:, :], w, xnT[b], start=True, stop=True).then_inc(full(f"{'qk'[i]}{b}"), 1)

            pe.wait_ge(consts_ready, 1)
            keep_clock(WARM_FIRST)
            turn_x(0)
            pe.wait_ge(small_loaded, 32)
            m = take("columns")
            nc.tensor.transpose(m[:, 0:E], gate_sb[:, :], identf[0:E, 0:E])
            pe.wait_ge(brow_turned, 1)
            for i in range(2):
                col = brow[:, i].rearrange("o d h -> o (d h)")
                mm = nc.tensor.matmul(m[:, E + i:E + i + 1], col, identf[0:1, 0:1], start=True, stop=True,
                                      skip_group_check=True)
            mm.then_inc(full("columns"), 1)
            keep_clock(WARM_SECOND)
            pe.wait_ge(wqk_turned, 1)
            for i in range(2):
                project_qk(0, i)

            def project_v(i):
                m = take(f"v{i}")
                if i == 0:
                    pe.wait_ge(wv_loaded, 16)
                    pe.wait_ge(wvg_ready, 1)
                for j in range(min(3, NT - 3 * i)):
                    t = 3 * i + j
                    if t % QT == 0:
                        wait_x_turned(pe, t // QT)
                    mm = nc.tensor.matmul(m[:, j * (D + E):(j + 1) * (D + E)],
                                          xnT[t // QT][:, t % QT * P:(t % QT + 1) * P], wvg[:, :],
                                          start=True, stop=True, skip_group_check=True)
                mm.then_inc(full(f"v{i}"), 1)

            for i in range(V_AHEAD):
                project_v(i)
            for b in range(1, B):
                turn_x(b)

            def count_ahead():
                pe.wait_ge(consts_ready, 2)
                pe.wait_ge(onehot_ready, 1)
                m = take("route")
                nc.tensor.matmul(m[:, 0:NT * E], before[:, :], onehot[:, :, :].rearrange("p t e -> p (t e)"),
                                 start=True, stop=False, skip_group_check=True)
                for t in range(NT - 1):
                    n = NT - 1 - t
                    mm = nc.tensor.matmul(m[:, (t + 1) * E:NT * E].rearrange("p (t e) -> p t e", e=E), onesb[:, :],
                                          onehot[:, t:t + 1, :].to_broadcast([P, n, E]), start=False,
                                          stop=(t == NT - 2), skip_group_check=True)
                mm.then_inc(full("route"), 1)

            def scores_by_query(k, i):
                b, g = divmod(k, NG)
                n = k * S1N + i
                if i == 0 and g == 0:
                    pe.wait_ge(parts_placed[b], 16 * placed_dmas(b))
                if n >= S1_BANKS:
                    pe.wait_ge(s1_free, n - S1_BANKS + 1)
                pt = s1_bank[n % S1_BANKS]
                blocks = query_blocks(g, i)
                w = (blocks[0][1] + 1) * P
                for j, (h, qt) in enumerate(blocks):
                    mm = nc.tensor.matmul(pt[:, j * w:(j + 1) * w], qs[:, b % 2, h, qt * P:(qt + 1) * P],
                                          ks[:, b % 2, h, 0:w], start=(j == 0), stop=(i < FUSED), skip_group_check=True)
                if i < FUSED:
                    mm.then_inc(s1_full, 1)
                    return
                c = len(blocks)
                diag = pt[:, 0:c * w].rearrange("p (c w) -> p c w", c=c)[:, :, w - P:w]
                neg = maskneg.rearrange("p (o k) -> p o k", o=1).to_broadcast([P, c, P])
                nc.tensor.matmul(diag, identb[:, :], neg, start=False, stop=True, skip_group_check=True)\
                    .then_inc(s1_full, 1)

            def scores_by_key(k, i):
                b, g = divmod(k, NG)
                n = k * S2N + i
                if i == 0:
                    pe.wait_ge(max_placed[k % 2], 16 * (k // 2 + 1))
                if n >= S2_BANKS:
                    pe.wait_ge(s2_free, n - S2_BANKS + 1)
                pt = s2_bank[n % S2_BANKS]
                h0 = g * G
                if i < G:
                    blocks = [(h0 + i, 0, 0)]
                elif i < 2 * G:
                    blocks = [(h0 + i - G, 1, 0), (h0 + i - G, 3, 3 * P)]
                else:
                    blocks = [(h0 + 2 * (i - 2 * G), 2, 0), (h0 + 2 * (i - 2 * G) + 1, 2, 2 * P)]
                for h, kb, at in blocks:
                    w = S - kb * P
                    mm = nc.tensor.matmul(pt[:, at:at + w], ks[:, b % 2, h, kb * P:(kb + 1) * P],
                                          qs[:, b % 2, h, kb * P:S], start=True, stop=True, skip_group_check=True)
                mm.then_inc(s2_full, 1)

            def probs_of(par, j, kb):
                if kb == 0:
                    return probs[:, par, j, :]
                if kb == 1:
                    return probs[:, par, G + j, 0:3 * P]
                if kb == 3:
                    return probs[:, par, G + j, 3 * P:4 * P]
                return probs[:, par, 2 * G + j // 2, (j % 2) * 2 * P:(j % 2 + 1) * 2 * P]

            def weigh_values(k, kb):
                b, g = divmod(k, NG)
                final = QT - 2 if k == K - 1 else QT - 1
                pe.wait_ge(s2_free, k * S2N + (G, 2 * G, S2N, 2 * G)[kb])
                pe.wait_ge(masked, 4 * k + (1, 2, 4, 3)[kb])
                if kb == 0:
                    if k == 0:
                        pe.wait_ge(o_filled, 1)
                    else:
                        pe.wait_ge(o_copied, k)
                for j in range(G):
                    mm = nc.tensor.matmul(o_bank[32 * j:32 * j + HD + 1, kb * P:S], v_aug[:, b * QT + kb, g * G + j, :],
                                          probs_of(k % 2, j, kb), start=(kb == 0), stop=(kb == final),
                                          skip_group_check=True)
                if kb == final:
                    mm.then_inc(weighed, 1)

            def turn_o(k):
                m = take(f"oT{k}")
                pe.wait_ge(o_copied, k + 1)
                for t in range(QT):
                    mm = nc.tensor.transpose(m[:, t * P:(t + 1) * P], oT_sb[:, k % 2, t * P:(t + 1) * P], identf[:, :])
                mm.then_inc(full(f"oT{k}"), 1)

            def sum_values(b):
                m = take(f"cum{b}")
                pe.wait_ge(vpre_ready, 2 * b + 2)
                va = v_aug[:, b * QT:(b + 1) * QT, :, 0:HD].rearrange("p t h d -> p (t h) d")
                nc.tensor.matmul(m[:, :], upto[:, :], va, start=True, stop=False, skip_group_check=True)
                nc.tensor.matmul(m[:, P:2 * P], onesf[:, :], va[:, 0:H, :], start=False, stop=False,
                                 skip_group_check=True)
                nc.tensor.matmul(m[:, 2 * P:4 * P], onesf[:, :], v_pre[:, :, :].rearrange("p t d -> p (t d)"),
                                 start=False, stop=True, skip_group_check=True).then_inc(full(f"cum{b}"), 1)

            def turn_max(k):
                m = take(f"maxT{k}")
                pe.wait_ge(s1_free, (k + 1) * S1N)
                nc.tensor.transpose(m[0:G * QT, 0:P], mx[:, k % 2].rearrange("p h t -> p (h t)"), identf[:, :])\
                    .then_inc(full(f"maxT{k}"), 1)

            def turn_blocks(name, source, at):
                m = take(name)
                for j in range(4):
                    mm = nc.tensor.transpose(m[:, j * P:(j + 1) * P], source(at + j), identf[:, :])
                mm.then_inc(full(name), 1)

            def expert_hidden(e, c):
                if c == 0:
                    pe.wait_ge(w_ring[e % WR], 32 * (e // WR + 1))
                    if e == 0:
                        for i in range(SB // 4):
                            wait_free(pe, f"slotT{i}")
                m = take(f"hid{e}_{c}")
                for j in range(2):
                    at = (2 * c + j) * P
                    mm = nc.tensor.matmul(m[:, j * CAP:(j + 1) * CAP], w1_sb[:, e % WR, at:at + P],
                                          slot_xT[:, e * CAP:(e + 1) * CAP], start=True, stop=True,
                                          skip_group_check=True)
                mm.then_inc(full(f"hid{e}_{c}"), 1)

            def expert_result(e):
                m = take(f"res{e}")
                for c in range(2):
                    wait_free(pe, f"hid{e}_{c}")
                for c in range(FC):
                    mm = nc.tensor.matmul(m[:, 0:CAP], w2_sb[:, e % WR, c, :], hid[:, e % 2, c, :],
                                          start=(c == 0), stop=(c == FC - 1))
                mm.then_inc(full(f"res{e}"), 1)

            def turn_attn(b, half=None):
                name, ts = share("attT", b, half)
                m = take(name)
                pe.wait_ge(attn_ready, (b + 1) * NG)
                for t in range(ts.start, ts.stop):
                    mm = nc.tensor.transpose(m[:, t * P:(t + 1) * P], attn[:, b * QT + t, :], identf[:, :])
                mm.then_inc(full(name), 1)

            def project_attn(b, half=None):
                name, ts = share("proj", b, half)
                m = take(name)
                wait_free(pe, share("attT", b, half)[0])
                if b == 0:
                    pe.wait_ge(wc_loaded, 16)
                for t in range(ts.start, ts.stop):
                    mm = nc.tensor.matmul(m[:, t * P:(t + 1) * P], att_T[:, t * P:(t + 1) * P], wc[:, :],
                                          start=True, stop=True, skip_group_check=True)
                mm.then_inc(full(name), 1)

            def part(k, kind, arg):
                if kind == "s2":
                    scores_by_key(k, arg)
                elif kind == "s1":
                    scores_by_query(*arg)
                elif kind == "v":
                    project_v(arg)
                elif kind == "count":
                    count_ahead()
                elif kind == "weigh":
                    weigh_values(*arg)
                elif kind == "qk":
                    project_qk(*arg)
                elif kind == "slotT":
                    pe.wait_ge(slots_loaded, 16)
                    turn_blocks(f"slotT{arg}", lambda s: slot_sb[:, s, :], 4 * arg)
                elif kind == "hid":
                    expert_hidden(*arg)
                elif kind == "res":
                    expert_result(arg)
                elif kind == "resT":
                    if arg == 0:
                        for e in (E - 2, E - 1):
                            wait_free(pe, f"res{e}")
                    turn_blocks(f"resT{arg}", lambda s: slot_xT[:, s * P:(s + 1) * P], 4 * arg)
                elif kind == "oT":
                    turn_o(arg)
                elif kind == "cum":
                    sum_values(arg)
                elif kind == "maxT":
                    turn_max(arg)
                elif kind == "attT":
                    turn_attn(arg)
                elif kind == "proj":
                    project_attn(arg)

            for k in STAGES:
                for kind, arg in orders[k]:
                    part(k, kind, arg)
            turn_o(K - 1)
            for half in range(2):
                turn_attn(B - 1, half)
            for half in range(2):
                project_attn(B - 1, half)

        @block.vector
        def _(dve):
            ln = [0]

            def ln_count(ins):
                ln[0] += 1
                ins.then_inc(ln_step, 1)
                return ln[0]

            def statistics(batches):
                tiles = range(batches[0] * QT, (batches[-1] + 1) * QT)
                ts = slice(tiles[0], tiles[-1] + 1)
                for t in tiles:
                    if t % QT == 0:
                        dve.wait_ge(x_loaded[t // QT], 16)
                    n = ln_count(nc.vector.bn_stats(stats[:, t, :], x_sb[:, t, :]))
                first = n - len(tiles) + 1
                for j, t in enumerate(tiles):
                    dve.wait_ge(ln_step, first + j)
                    n = ln_count(nc.vector.bn_aggr(mv[:, t, :], stats[:, t, :]))
                dve.wait_ge(ln_step, n)
                nc.vector.tensor_scalar(rstd[:, 0, ts], mv[:, ts, 1], 1e-5, None, ALU.add).then_inc(var_ready, 1)

            def deviations(batches):
                ts = slice(batches[0] * QT, (batches[-1] + 1) * QT)
                turn = 0 if batches[0] == 0 else 1
                dve.wait_ge(std_ready, turn + 1)
                n = ln_count(nc.vector.reciprocal(rstd[:, 2, ts], rstd[:, 1, ts]))
                dve.wait_ge(ln_step, n)
                n = ln_count(nc.vector.tensor_tensor(rstd[:, 1, ts], rstd[:, 2, ts], rstd[:, 2, ts], ALU.mult))
                dve.wait_ge(ln_step, n)
                n = ln_count(nc.vector.tensor_tensor(rstd[:, 3, ts], rstd[:, 1, ts], rstd[:, 0, ts], ALU.mult))
                dve.wait_ge(ln_step, n)
                n = ln_count(nc.vector.tensor_scalar(rstd[:, 1, ts], rstd[:, 3, ts], -0.5, 1.5, ALU.mult, ALU.add))
                dve.wait_ge(ln_step, n)
                nc.vector.tensor_tensor(rstd[:, 0, ts], rstd[:, 2, ts], rstd[:, 1, ts], ALU.mult).then_inc(rstd_ready, 1)

            def split_rest(b, i):
                m = wait_full(dve, f"{'qk'[i]}{b}")
                dve.wait_ge(hi_ready, 2 * b + i + 1)
                nc.vector.scalar_tensor_tensor(out=rest[:, i, :], in0=m[:, :], scalar=bias[:, i:i + 1],
                                               in1=parts[:, i, 0, :], op0=ALU.add, op1=ALU.subtract)\
                    .then_inc(free(f"{'qk'[i]}{b}"), 1)

            def normalise_x(b):
                dve.wait_ge(rstd_ready, 2 if b else 1)
                for t in range(b * QT, (b + 1) * QT):
                    ins = nc.vector.tensor_scalar(xn[:, t, :], x_sb[:, t, :], mv[:, t, 0:1], rstd[:, 0, t:t + 1],
                                                  ALU.subtract, ALU.mult)
                ins.then_inc(xn_ready[b], 1)

            statistics(range(1))
            deviations(range(1))
            normalise_x(0)
            statistics(range(1, B))
            for i in range(2):
                split_rest(0, i)
            deviations(range(1, B))
            split_lo(dve, nc.vector, 0)
            for b in range(1, B):
                normalise_x(b)
            nc.vector.memset(o_bank[:, :], 0.0).then_inc(o_filled, 1)

            def by_token(v):
                return v.rearrange("p (t o) -> p t o", o=1).to_broadcast([P, NT, E])

            def by_expert(v):
                return v.rearrange("p (o e) -> p o e", o=1).to_broadcast([P, NT, E])

            def choose_experts(j):
                if j == 0:
                    for i in (VB - 2, VB - 1):
                        wait_free(dve, f"v{i}")
                    nc.vector.tensor_reduce(rtc[:, 0, :], lg[:, :, :], AX.X, ALU.max).then_inc(route_step, 1)
                elif j == 1:
                    dve.wait_ge(route_step, 1)
                    nc.vector.tensor_tensor(rt[:, 0], lg[:, :, :], by_token(rtc[:, 0, :]), ALU.subtract)\
                        .then_inc(gate_shift_ready, 1)
                    nc.vector.tensor_tensor(rt[:, 2], lg[:, :, :], by_token(rtc[:, 0, :]), ALU.is_equal)\
                        .then_inc(route_step, 1)
                elif j == 2:
                    dve.wait_ge(route_step, 2)
                    dve.wait_ge(consts_ready, 2)
                    nc.vector.scalar_tensor_tensor(out=lg[:, :, :], in0=rt[:, 2], scalar=-float(E), in1=by_expert(ev[:, :]),
                                                   op0=ALU.mult, op1=ALU.add).then_inc(route_step, 1)
                elif j == 3:
                    dve.wait_ge(route_step, 3)
                    nc.vector.tensor_reduce(rtc[:, 1, :], lg[:, :, :], AX.X, ALU.min).then_inc(route_step, 1)
                elif j == 4:
                    dve.wait_ge(route_step, 4)
                    nc.vector.tensor_scalar(rtc[:, 3, :], rtc[:, 1, :], float(E), None, ALU.add).then_inc(route_step, 1)
                else:
                    dve.wait_ge(route_step, 5)
                    nc.vector.tensor_tensor(onehot[:, :, :], by_expert(ev[:, :]), by_token(rtc[:, 3, :]), ALU.is_equal)\
                        .then_inc(onehot_ready, 1)

            def number_slots(j):
                if j == 0:
                    dve.wait_ge(onehot_ready, 1)
                    m = wait_full(dve, "route")
                    nc.vector.tensor_tensor(rt[:, 2], m[:, 0:NT * E].rearrange("p (t e) -> p t e", e=E), onehot[:, :, :],
                                            ALU.mult).then_inc(free("route"), 1)
                elif j == 1:
                    wait_free(dve, "route")
                    nc.vector.tensor_reduce(rtc[:, 5, :], rt[:, 2], AX.X, ALU.add).then_inc(route_step, 1)
                elif j == 2:
                    dve.wait_ge(route_step, 6)
                    nc.vector.tensor_scalar(rtc[:, 6, :], rtc[:, 5, :], float(CAP), DROPPED, ALU.is_ge, ALU.mult)\
                        .then_inc(route_step, 1)
                    nc.vector.scalar_tensor_tensor(out=rtc[:, 7, :], in0=rtc[:, 3, :], scalar=float(CAP),
                                                   in1=rtc[:, 5, :], op0=ALU.mult, op1=ALU.add).then_inc(route_step, 1)
                elif j == 3:
                    dve.wait_ge(route_step, 8)
                    nc.vector.tensor_tensor(rtc[:, 5, :], rtc[:, 7, :], rtc[:, 6, :], ALU.add).then_inc(route_step, 1)
                else:
                    dve.wait_ge(route_step, 9)
                    nc.vector.tensor_scalar(idx[:, :], rtc[:, 5, :], float(E * CAP), None, ALU.add).then_inc(idx_ready, 1)

            def find_weights(j):
                if j == 0:
                    dve.wait_ge(gate_exp_ready, 1)
                    nc.vector.tensor_reduce(rtc[:, 4, :], rt[:, 1], AX.X, ALU.add).then_inc(route_step, 1)
                    dve.wait_ge(gains_loaded, 48)
                    nc.vector.tensor_copy(inv_row[:, 0, :], row_i[:, :]).then_inc(cum_gain_step, 1)
                elif j == 1:
                    dve.wait_ge(route_step, 10)
                    nc.vector.reciprocal(rtc[:, 2, :], rtc[:, 4, :]).then_inc(prob_ready, 1)
                    dve.wait_ge(cum_gain_step, 1)
                    nc.vector.reciprocal(inv_row[:, 1, :], inv_row[:, 0, :]).then_inc(cum_gain_step, 1)
                else:
                    dve.wait_ge(cum_gain_step, 2)
                    nc.vector.tensor_tensor(cum_gain[:, :, :],
                                            inv_row[:, 1, :].rearrange("p (t o) -> p t o", o=1).to_broadcast([P, QT, H]),
                                            gains[:, 2, :].rearrange("p (o h) -> p o h", o=1).to_broadcast([P, QT, H]),
                                            ALU.mult).then_inc(cum_gain_step, 1)

            def row_maxima(k, i):
                n = k * S1N + i
                dve.wait_ge(s1_full, n + 1)
                blocks = query_blocks(0, i)
                w = (blocks[0][1] + 1) * P
                h0, qt = blocks[0]
                c = len(blocks)
                if i < FUSED:
                    for j, (h, qt) in enumerate(blocks):
                        bank = s1_bank[n % S1_BANKS][:, j * w:(j + 1) * w]
                        ins = nc.vector.tensor_tensor_reduce(bank, bank, causal[:, S - w:S], 1.0, NEG, ALU.add, ALU.max,
                                                             mx[:, k % 2, h, qt:qt + 1])
                    ins.then_inc(s1_free, 1)
                    return
                blocks = s1_bank[n % S1_BANKS][:, 0:c * w].rearrange("p (c w) -> p c w", c=c)
                nc.vector.tensor_reduce(mx[:, k % 2, h0:h0 + c, qt], blocks, AX.X, ALU.max).then_inc(s1_free, 1)

            def normalise(k):
                b, g = divmod(k, NG)
                m = wait_full(dve, f"oT{k}")
                ov = m[:, :].rearrange("p (t j r) -> p t j r", t=QT, j=G)
                nc.vector.reciprocal(rec[:, :, :], ov[:, :, :, HD]).then_inc(norm_step, 1)
                dve.wait_ge(norm_step, 2 * k + 1)
                gain = gains[:, 0, g * G:(g + 1) * G].rearrange("p (o j) -> p o j", o=1).to_broadcast([P, QT, G])
                nc.vector.tensor_tensor(recg[:, :, :], rec[:, :, :], gain, ALU.mult).then_inc(norm_step, 1)
                dve.wait_ge(norm_step, 2 * k + 2)
                weight = recg[:, :, :].rearrange("p t (j o) -> p t j o", o=1).to_broadcast([P, QT, G, HD])
                nc.vector.tensor_tensor(onorm[:, :, :, :], ov[:, :, :, 0:HD], weight, ALU.mult).then_inc(free(f"oT{k}"), 1)
                wait_free(dve, f"oT{k}")
                if g == 0:
                    dve.wait_ge(base_ready, b + 1)
                av = attn[:, b * QT:(b + 1) * QT, g * G * HD:(g + 1) * G * HD].rearrange("p t (j d) -> p t j d", j=G)
                nc.vector.tensor_tensor(av, av, onorm[:, :, :, :], ALU.add).then_inc(attn_ready, 1)

            def take_off_means(b):
                m = wait_full(dve, f"cum{b}")
                gain = cum_gain[:, :, :].rearrange("p t h -> p (t h)").rearrange("p (n o) -> p n o", o=1)\
                    .to_broadcast([P, QT * H, HD])
                if b == 0:
                    dve.wait_ge(cum_gain_step, 3)
                nc.vector.tensor_tensor(cum_part[:, :, :, :].rearrange("p t h d -> p (t h) d"),
                                        m[:, :].rearrange("p (n d) -> p n d", d=HD), gain, ALU.mult)\
                    .then_inc(free(f"cum{b}"), 1)
                wait_free(dve, f"cum{b}")
                dve.wait_ge(skip_ready, b + 1)
                av = attn[:, b * QT:(b + 1) * QT, :].rearrange("p t d -> p (t d)")
                nc.vector.tensor_tensor(av, av, cum_part[:, :, :, :].rearrange("p t h d -> p (t h d)"), ALU.subtract)\
                    .then_inc(base_ready, 1)

            def finish(b, half=None):
                name, ts = share("proj", b, half)
                m = wait_full(dve, name)
                dve.wait_ge(silu_ready, b + 1)
                if b >= 2:
                    dve.wait_ge(y_stored[b % 2], 16 * (b // 2))
                cols = slice(ts.start * P, ts.stop * P)
                tiles = slice(b * QT + ts.start, b * QT + ts.stop)
                nc.vector.tensor_tensor(y_sb[:, b % 2, cols], m[:, cols], fg[:, tiles, :].rearrange("p t d -> p (t d)"),
                                        ALU.mult).then_inc(free(name), 1)
                wait_free(dve, name)
                nc.vector.tensor_tensor(y_sb[:, b % 2, cols], y_sb[:, b % 2, cols],
                                        x_sb[:, tiles, :].rearrange("p t d -> p (t d)"), ALU.add).then_inc(y_ready, 1)

            def part(k, kind, arg):
                if kind == "s1":
                    row_maxima(*arg)
                elif kind == "choose":
                    choose_experts(arg)
                elif kind == "number":
                    number_slots(arg)
                elif kind == "find":
                    find_weights(arg)
                elif kind == "qk":
                    split_rest(*arg)
                elif kind == "res":
                    m = wait_full(dve, f"res{arg}")
                    nc.vector.tensor_copy(slot_xT[:, arg * CAP:(arg + 1) * CAP], m[:, 0:CAP]).then_inc(free(f"res{arg}"), 1)
                elif kind == "resT":
                    m = wait_full(dve, f"resT{arg}")
                    nc.vector.tensor_copy(slot_sb[:, 4 * arg:4 * arg + 4, :].rearrange("p k d -> p (k d)"), m[:, :])\
                        .then_inc(free(f"resT{arg}"), 1)
                elif kind == "oT":
                    normalise(arg)
                elif kind == "cum":
                    take_off_means(arg)
                elif kind == "maxT":
                    m = wait_full(dve, f"maxT{arg}")
                    dve.wait_ge(nm_hi_ready, arg + 1)
                    nc.vector.scalar_tensor_tensor(out=mrest[:, :], in0=m[0:G * QT, 0:P], scalar=-1.0,
                                                   in1=negm[:, arg % 2, 0, :], op0=ALU.mult, op1=ALU.subtract)\
                        .then_inc(free(f"maxT{arg}"), 1)
                elif kind == "max_low":
                    dve.wait_ge(nm_mid_ready, arg + 1)
                    nc.vector.tensor_tensor(negm[:, arg % 2, 2, :], mrest[:, :], negm[:, arg % 2, 1, :], ALU.subtract)\
                        .then_inc(nm_lo_ready, 1)
                elif kind == "proj":
                    finish(arg)
                elif kind == "copy_o" and k + LAG >= K:
                    copy_o(dve, arg)
                elif kind == "attT" and k + LAG >= K:
                    copy_attT(dve, arg)

            for k in STAGES:
                for kind, arg in orders[k]:
                    part(k, kind, arg)
            normalise(K - 1)
            copy_attT(dve, B - 1, 1)
            for half in range(2):
                finish(B - 1, half)


_INS = ["L0_attn_x", "L0_attn_qk_w", "L0_attn_qk_b", "L0_attn_v_w", "L0_attn_cproj_w", "L0_attn_resid_gain",
        "L0_attn_skip_gain", "L0_attn_centre_gain", "L0_ffn_gate_w", "L0_ffn_w1", "L0_ffn_w2"]


def kernel(**inputs):
    import numpy as _np
    import concourse.bacc as _bacc
    from concourse import mybir as _mybir
    from concourse.bass_utils import run_bass_kernel_spmd as _run

    nc = _bacc.Bacc("TRN2", target_bir_lowering=False, num_devices=1)
    arrays, args = {}, []
    for name in _INS:
        a = _np.ascontiguousarray(inputs[name])
        arrays[f"in_{name}"] = a
        args.append(nc.dram_tensor(f"in_{name}", a.shape, _mybir.dt.from_np(a.dtype), kind="ExternalInput").ap())
    shape = inputs["L0_attn_x"].shape
    args.append(nc.dram_tensor("out_0", shape, _mybir.dt.float32, kind="ExternalOutput").ap())
    attention_moe_block(nc, *args)
    r = _run(nc, [arrays], core_ids=[0])
    return r.results[0]["out_0"]
```
